# Optimizing a Trainium2 kernel written in Bass

```python
import numpy as np
import jax
import jax.numpy as jnp

def _softmax(x, axis=-1):
    return jax.nn.softmax(x, axis=axis)

def _gelu(x):
    return jax.nn.gelu(x, approximate=True)

def _silu(x):
    return jax.nn.silu(x)

def _sigmoid(x):
    return jax.nn.sigmoid(x)

def _layernorm(x, axis=-1, eps=1e-05):
    m = jnp.mean(x, axis=axis, keepdims=True)
    v = jnp.var(x, axis=axis, keepdims=True)
    return (x - m) / jnp.sqrt(v + eps)

def _scatter_add(tgt, idx, src, axis=0):
    return tgt.at[idx].add(src)

def _segment_sum(src, seg, n):
    return jax.ops.segment_sum(src, seg, n)
kernel_name = 'mk_prb_d1_jaxref_r8_f35b9a'

def setup_inputs(seed: int=0):
    np.random.seed(seed)
    _w = jnp.asarray

    def _L0_attn_setup():
        import jax, jax.numpy as jnp
        import numpy as np
        from jax import lax
        D_MODEL = 128
        N_HEADS = 4
        D_STATE = 64
        D_CONV = 4
        EXPAND = 2
        D_INNER = EXPAND * D_MODEL
        DT_RANK = 64
        H_DIN = D_INNER // N_HEADS
        H_DT = DT_RANK // N_HEADS
        H_DS = D_STATE // N_HEADS
        BATCH, SEQ = (2, 128)
        key = jax.random.key(seed)
        ks = jax.random.split(key, 8)
        hidden_states = jax.random.normal(ks[0], (BATCH, SEQ, D_MODEL), dtype=jnp.float32)
        s_in = 1.0 / np.sqrt(D_MODEL)
        in_proj_w = jax.random.uniform(ks[1], (2 * D_INNER, D_MODEL), minval=-s_in, maxval=s_in)
        s_c = 1.0 / np.sqrt(D_CONV)
        conv_w = jax.random.uniform(ks[2], (D_INNER, 1, D_CONV), minval=-s_c, maxval=s_c)
        conv_b = jax.random.uniform(ks[3], (D_INNER,), minval=-s_c, maxval=s_c)
        s_x = 1.0 / np.sqrt(H_DIN)
        x_proj_w = jax.random.uniform(ks[4], ((2 * H_DS + H_DT) * N_HEADS, H_DIN), minval=-s_x, maxval=s_x)
        s_dt = H_DT ** (-0.5)
        dt_proj_w = jax.random.uniform(ks[5], (D_INNER, H_DT), minval=-s_dt, maxval=s_dt)
        dt = jnp.exp(jax.random.uniform(ks[6], (D_INNER,)) * (np.log(0.1) - np.log(0.001)) + np.log(0.001))
        dt = jnp.clip(dt, 0.0001, None)
        dt_proj_b = dt + jnp.log(-jnp.expm1(-dt))
        A_log = jnp.log(jnp.tile(jnp.arange(1, H_DS + 1, dtype=jnp.float32), (D_INNER, 1)))
        Dskip = jnp.ones((D_INNER,), dtype=jnp.float32)
        out_proj_w = jax.random.uniform(ks[7], (D_MODEL, D_INNER), minval=-s_x, maxval=s_x)
        return {'hidden_states': hidden_states, 'in_proj_w': in_proj_w, 'conv_w': conv_w, 'conv_b': conv_b, 'x_proj_w': x_proj_w, 'dt_proj_w': dt_proj_w, 'dt_proj_b': dt_proj_b, 'A_log': A_log, 'Dskip': Dskip, 'out_proj_w': out_proj_w}
    _L0_attn_in = _L0_attn_setup()

    def _L0_ffn_setup():
        import jax, jax.numpy as jnp
        import numpy as np

        def _moe_forward(x, Wg, W1, b1, W2, b2):
            B, S, H = x.shape
            E = Wg.shape[1]
            tokens = x.reshape(-1, H)
            T = tokens.shape[0]
            C = -(-T // E)
            logits = tokens @ Wg
            gates = jax.nn.softmax(logits, axis=-1)
            idx = jnp.argmax(gates, axis=1)
            mask1 = jax.nn.one_hot(idx, E, dtype=gates.dtype)
            locations1 = jnp.cumsum(mask1, axis=0) - 1.0
            mask1 = mask1 * (locations1 < C).astype(gates.dtype)
            loc_s = jnp.sum(locations1 * mask1, axis=1).astype(jnp.int32)
            gates1 = jnp.sum(gates * mask1, axis=1)
            loc_oh = jax.nn.one_hot(loc_s, C, dtype=gates.dtype)
            dispatch = mask1[:, :, None] * loc_oh[:, None, :]
            combine = gates1[:, None, None] * dispatch
            expert_in = jnp.einsum('tec,th->ech', dispatch, tokens)
            hidden = jax.nn.relu(jnp.einsum('ech,ehf->ecf', expert_in, W1) + b1[:, None, :])
            expert_out = jnp.einsum('ecf,efh->ech', hidden, W2) + b2[:, None, :]
            out = jnp.einsum('tec,ech->th', combine, expert_out)
            return out.reshape(B, S, H)
        key = jax.random.key(seed)
        ks = jax.random.split(key, 6)
        B, S, H, F, E = (4, 256, 128, 512, 8)
        x = jax.random.normal(ks[0], (B, S, H), dtype=jnp.float32)
        Wg = jax.random.normal(ks[1], (H, E), dtype=jnp.float32) * (1.0 / np.sqrt(H))
        W1 = jax.random.normal(ks[2], (E, H, F), dtype=jnp.float32) * (1.0 / np.sqrt(H))
        b1 = jnp.zeros((E, F), dtype=jnp.float32)
        W2 = jax.random.normal(ks[3], (E, F, H), dtype=jnp.float32) * (1.0 / np.sqrt(F))
        b2 = jnp.zeros((E, H), dtype=jnp.float32)
        return {'x': x, 'Wg': Wg, 'W1': W1, 'b1': b1, 'W2': W2, 'b2': b2}
    _L0_ffn_in = _L0_ffn_setup()
    _d = {'L0_attn_hidden_states': _L0_attn_in['hidden_states'], 'L0_attn_in_proj_w': _L0_attn_in['in_proj_w'], 'L0_attn_conv_w': _L0_attn_in['conv_w'], 'L0_attn_conv_b': _L0_attn_in['conv_b'], 'L0_attn_x_proj_w': _L0_attn_in['x_proj_w'], 'L0_attn_dt_proj_w': _L0_attn_in['dt_proj_w'], 'L0_attn_dt_proj_b': _L0_attn_in['dt_proj_b'], 'L0_attn_A_log': _L0_attn_in['A_log'], 'L0_attn_Dskip': _L0_attn_in['Dskip'], 'L0_attn_out_proj_w': _L0_attn_in['out_proj_w'], 'L0_ffn_Wg': _L0_ffn_in['Wg'], 'L0_ffn_W1': _L0_ffn_in['W1'], 'L0_ffn_b1': _L0_ffn_in['b1'], 'L0_ffn_W2': _L0_ffn_in['W2'], 'L0_ffn_b2': _L0_ffn_in['b2']}
    _x0 = _d['L0_attn_hidden_states']
    _d['L0_attn_hidden_states'] = jax.random.normal(jax.random.fold_in(jax.random.key(seed), 1), (32, 256, 128), dtype=_x0.dtype)
    del _x0
    return _d

def reference(L0_attn_hidden_states, L0_attn_in_proj_w, L0_attn_conv_w, L0_attn_conv_b, L0_attn_x_proj_w, L0_attn_dt_proj_w, L0_attn_dt_proj_b, L0_attn_A_log, L0_attn_Dskip, L0_attn_out_proj_w, L0_ffn_Wg, L0_ffn_W1, L0_ffn_b1, L0_ffn_W2, L0_ffn_b2):

    def _L0_attn_ref(hidden_states, in_proj_w, conv_w, conv_b, x_proj_w, dt_proj_w, dt_proj_b, A_log, Dskip, out_proj_w):
        import jax, jax.numpy as jnp
        import numpy as np
        from jax import lax
        D_MODEL = 128
        N_HEADS = 4
        D_STATE = 64
        D_CONV = 4
        EXPAND = 2
        D_INNER = EXPAND * D_MODEL
        DT_RANK = 64
        H_DIN = D_INNER // N_HEADS
        H_DT = DT_RANK // N_HEADS
        H_DS = D_STATE // N_HEADS
        BATCH, SEQ = (2, 128)
        b, L, _ = hidden_states.shape
        xz = hidden_states @ in_proj_w.T
        x, z = jnp.split(xz, 2, axis=-1)
        xp = jnp.pad(x, ((0, 0), (D_CONV - 1, 0), (0, 0)))
        w = conv_w[:, 0, :]
        xc = conv_b
        for k in range(D_CONV):
            xc = xc + xp[:, k:k + L, :] * w[:, k]
        x = jax.nn.silu(xc)
        xh = x.reshape(b, L, N_HEADS, H_DIN)
        xw = x_proj_w.reshape(N_HEADS, 2 * H_DS + H_DT, H_DIN)
        x_dbl = jnp.einsum('hod,blhd->blho', xw, xh)
        dt_r, Bm, Cm = jnp.split(x_dbl, [H_DT, H_DT + H_DS], axis=-1)
        dtw = dt_proj_w.reshape(N_HEADS, H_DIN, H_DT)
        delta = jnp.einsum('hdr,blhr->blhd', dtw, dt_r)
        delta = jax.nn.softplus(delta + dt_proj_b.reshape(N_HEADS, H_DIN))
        A = -jnp.exp(A_log).reshape(N_HEADS, H_DIN, H_DS)

        def step(s, inp):
            d_t, u_t, B_t, C_t = inp
            dA = jnp.exp(d_t[..., None] * A)
            s = s * dA + (d_t * u_t)[..., None] * B_t[:, :, None, :]
            y_t = jnp.einsum('bhdn,bhn->bhd', s, C_t)
            return (s, y_t)
        s0 = jnp.zeros((b, N_HEADS, H_DIN, H_DS), dtype=x.dtype)
        scan_in = (delta.transpose(1, 0, 2, 3), xh.transpose(1, 0, 2, 3), Bm.transpose(1, 0, 2, 3), Cm.transpose(1, 0, 2, 3))
        _, ys = lax.scan(step, s0, scan_in)
        y = ys.transpose(1, 0, 2, 3).reshape(b, L, D_INNER)
        y = y + x * Dskip
        y = y * jax.nn.silu(z)
        out = y @ out_proj_w.T
        return out

    def _L0_ffn_ref(x, Wg, W1, b1, W2, b2):
        import jax, jax.numpy as jnp
        import numpy as np

        def _moe_forward(x, Wg, W1, b1, W2, b2):
            B, S, H = x.shape
            E = Wg.shape[1]
            tokens = x.reshape(-1, H)
            T = tokens.shape[0]
            C = -(-T // E)
            logits = tokens @ Wg
            gates = jax.nn.softmax(logits, axis=-1)
            idx = jnp.argmax(gates, axis=1)
            mask1 = jax.nn.one_hot(idx, E, dtype=gates.dtype)
            locations1 = jnp.cumsum(mask1, axis=0) - 1.0
            mask1 = mask1 * (locations1 < C).astype(gates.dtype)
            loc_s = jnp.sum(locations1 * mask1, axis=1).astype(jnp.int32)
            gates1 = jnp.sum(gates * mask1, axis=1)
            loc_oh = jax.nn.one_hot(loc_s, C, dtype=gates.dtype)
            dispatch = mask1[:, :, None] * loc_oh[:, None, :]
            combine = gates1[:, None, None] * dispatch
            expert_in = jnp.einsum('tec,th->ech', dispatch, tokens)
            hidden = jax.nn.relu(jnp.einsum('ech,ehf->ecf', expert_in, W1) + b1[:, None, :])
            expert_out = jnp.einsum('ecf,efh->ech', hidden, W2) + b2[:, None, :]
            out = jnp.einsum('tec,ech->th', combine, expert_out)
            return out.reshape(B, S, H)
        return _moe_forward(x, Wg, W1, b1, W2, b2)
    x = L0_attn_hidden_states
    xn = _layernorm(x, axis=-1)
    x = x + _L0_attn_ref(xn, L0_attn_in_proj_w, L0_attn_conv_w, L0_attn_conv_b, L0_attn_x_proj_w, L0_attn_dt_proj_w, L0_attn_dt_proj_b, L0_attn_A_log, L0_attn_Dskip, L0_attn_out_proj_w) + _L0_ffn_ref(xn, L0_ffn_Wg, L0_ffn_W1, L0_ffn_b1, L0_ffn_W2, L0_ffn_b2)
    return x

_drawn_inputs = setup_inputs


def setup_inputs(seed=0):
    import zlib

    import numpy as np

    out = dict(_drawn_inputs(seed))
    spreads = {'L0_attn_Dskip': (1.0, 0.6), 'L0_ffn_b1': (0.0, 0.307), 'L0_ffn_b2': (0.0, 0.1)}
    factors = {'L0_attn_x_proj_w': 8.0,
     'L0_attn_dt_proj_w': 8.0,
     'L0_attn_dt_proj_b': 8.0,
     'L0_attn_A_log': 8.0}
    for name, (base, spread) in spreads.items():
        noise = np.random.default_rng([zlib.crc32(name.encode()), seed]).standard_normal(out[name].shape)
        drawn = base * np.exp(spread * noise) if base else spread * noise
        out[name] = jnp.asarray(drawn.astype(out[name].dtype))
    for name, factor in factors.items():
        out[name] = (out[name] * factor).astype(out[name].dtype)
    return out
```

```python
import concourse.bass as bass
from concourse import mybir
from contextlib import ExitStack

F32 = mybir.dt.float32
F32R = mybir.dt.float32r
U32 = mybir.dt.uint32
ALU = mybir.AluOpType
ACT = mybir.ActivationFunctionType
AX = mybir.AxisListType.X

P = 128
BATCH, SEQ, DM = 32, 256, 128
TOK = BATCH * SEQ
TILES = TOK // P
DIN, HEADS, HD, NS, RANK, TAPS = 256, 4, 64, 16, 16, 4
HALVES = DIN // P
CH = 512
CHUNKS = TOK // CH
SEQS = CH // SEQ
CT = CH // P
ROW = SEQ + TAPS - 1
UNITS = 16
SLOTS = HALVES * UNITS
RING = 4
EXP, FF = 8, 512
CAP = TOK // EXP
FT = FF // P
LN_BLK = 4
BT = TILES // LN_BLK
GROUP = 8
FIRST_FFN, FIRST_COMBINE = 1, 9
EPS = 1e-5
W_LOADS = 10 + 2 * HEADS
LOG_T = 1.0 / 16
LOG_C = (1.0, -0.49998897314071655, 0.3324422836303711, -0.22668342292308807)
K_ID, K_I2, K_TRI, K_ONE, K_FIRST, K_TRASH, K_KEEP, K_BASE = 0, 128, 192, 320, 448, 456, 520, 1032
K_COLS = K_TRI
K_ALL = K_BASE + EXP * TILES


def bass_mamba_moe(nc, hidden, in_w, conv_w, conv_b, xp_w, dt_w, dt_b, a_log, d_skip, out_w,
                   wg, w1, b1, w2, b2, consts, out):
    ctx = ExitStack()
    with ctx:
        def sb(name, shape, dt=F32):
            return ctx.enter_context(nc.sbuf_tensor(name, shape, dt))

        def sem(name):
            return ctx.enter_context(nc.semaphore(name))

        ein = nc.dram_tensor("expert_in", [2 * TOK, DM], F32, kind="Internal").ap()
        eout = nc.dram_tensor("expert_out", [TOK, DM], F32, kind="Internal").ap()

        acc = sb("acc", [P, TILES, DM])
        xn_pool = sb("xn", [P, TILES * DM])
        xn = xn_pool[:, :].rearrange("p (i d) -> p i d", d=DM)
        xnT = sb("xnT", [P, BATCH, ROW])
        con = sb("con", [P, K_COLS])
        ident = con[:, K_ID:K_ID + P]
        sel = sb("sel", [P, 32, 2, HD], F32R)
        wx = sb("wx", [P, HALVES, TAPS, P])
        wzo = sb("wzo", [P, 4, P])
        wz, wo = wzo[:, 0:2, :], wzo[:, 2:4, :]
        weff = sb("weff", [P, HALVES, P])
        bcw = sb("bcw", [P, HALVES, P])
        wg_sb = sb("wg_sb", [P, EXP])
        b1c = sb("b1c", [P, EXP * FT])
        b1_now = sb("b1_now", [P, FT])
        small = sb("small", [P, 64])
        cw = small[:, 0:8].rearrange("p (h k) -> p h k", h=HALVES)
        cb, dtb, dsk = small[:, 8:10], small[:, 10:12], small[:, 12:14]
        logc3 = small[:, 14:15]
        a_neg = sb("a_neg", [P, HEADS, NS // 2])
        spot = [0]

        def over_xn(n):
            spot[0] += n
            return xn_pool[:, spot[0] - n:spot[0]]

        w1_sb = over_xn(FF)
        w2_sb = over_xn(FT * DM).rearrange("p (f m) -> p f m", f=FT)
        xe = over_xn(CAP).rearrange("p (i d) -> p i d", d=DM)
        xeT = over_xn(CAP)
        hT = over_xn(FT * CH).rearrange("p (f t) -> p f t", f=FT)
        eo = over_xn(2 * CH).rearrange("p (h i d) -> p h i d", h=2, d=DM)
        back = over_xn(GROUP * DM).rearrange("p (i d) -> p i d", d=DM)
        b2_bc = over_xn(EXP * DM).rearrange("p (e d) -> p e d", d=DM)
        xs = sb("xs", [P, 2, HALVES, CH])
        zs = sb("zs", [P, 2, HALVES, CH])
        bc = sb("bc", [P, HALVES, CH], F32R)
        bc_f = bc[:, :, :].bitcast(F32)
        sp_e, sp_r, sp_l, sp_q = [sb(f"sp_{n}", [P, CH]) for n in "erlq"]
        sp_m = sb("sp_m", [P, CH // 2])
        sp_mask = sp_m[:, :].bitcast(mybir.dt.uint16)
        dd = sb("dd", [P, 2, CH])
        drep = sb("drep", [P, HALVES, 2, 2, CH])
        b_sb = sb("b_sb", [P, RING, CH])
        u_sb = sb("u_sb", [P, RING, CH])
        s_sb = sb("s_sb", [P, RING, CH])
        p_sb = sb("p_sb", [P, RING, CH])
        g_sb = sb("g_sb", [P, HALVES, CH])
        w_nat = b_sb[:, :, :].rearrange("p r (a m) -> p (r a) m", m=DM)
        wt = p_sb[:, 0:2, :].rearrange("p r (a m) -> p (r a) m", m=DM)
        wo_nat = s_sb[:, 0, 0:DIN]
        xin = s_sb[:, 0, DIN:DIN + 2 * P].rearrange("p (h d) -> p h d", h=2)
        dt_nat = s_sb[:, 1, 0:2 * RANK].rearrange("p (h r) -> p h r", h=2)
        b1_nat = s_sb[0:EXP * FT, 1, 32:32 + P]
        x_dt = s_sb[0:RANK, 1, 160:160 + HEADS * HD].rearrange("p (h d) -> p h d", h=HEADS)
        dtT = dd[0:RANK, 0, 0:DIN].rearrange("p (h d) -> p h d", h=HALVES)
        zero = dd[:, 1, 0:DM]
        squares = [u_sb[:, :, :], drep[:, 0, :, :, :].rearrange("p a b t -> p (a b) t")]
        ln = sp_m[:, 0:4 * TILES].rearrange("p (n i) -> p n i", n=4)
        mean, var, rstd, ln_t = (ln[:, n, :] for n in range(4))
        rt_a, rt_b = xs[:, 1, 0, :], xs[:, 1, 1, :]
        rt_hot, rt_pos = zs[:, 1, 0, :], zs[:, 1, 1, :]
        rt_tot = g_sb[:, 0, :]
        r_con = g_sb[:, 1, 0:K_KEEP - K_TRI]
        tri, ones = r_con[:, 0:P], r_con[:, P:2 * P]
        first_won, trash = r_con[:, K_FIRST - K_TRI:K_TRASH - K_TRI], r_con[:, K_TRASH - K_TRI:]
        keep, first_row = p_sb[:, 2, :], p_sb[:, 3, :]
        rt = s_sb[:, 2, 0:5 * TILES].rearrange("p (n i) -> p n i", n=5)
        r_max, r_sum, r_kept, r_slot, r_t = (rt[:, n, :] for n in range(5))
        gate = sb("gate", [P, TILES])[:, :]
        put_at = sb("put_at", [P, TILES], U32)
        take_at = sb("take_at", [P, TILES], U32)
        take_now = sb("take_now", [P, GROUP], U32)

        bank = [ctx.enter_context(nc.psum_tensor(f"bank{i}", [P, CH], F32)) for i in range(8)]
        decay = bank[0:2]
        b_ps = bank[2]
        c_ps = bank[3:5]
        y_ps = bank[5]
        misc = bank[6:8]

        S = {n: sem(n) for n in (
            "x_loaded0 x_loaded1 x_loaded2 x_loaded3 con_loaded w_loaded xin_zeroed xin_loaded "
            "setup_dve setup_pe setup_act a_ready zero_ready ein_zeroed "
            "ln_dve ln_act xn_ready xnT_pe xnT_act logits_pe route_dve route_act route_pe routed "
            "scattered b_bcast b_copied u_ready decay_ready scan_done c_bcast p_ready sum_done "
            "y_read g_ready misc_pe misc_act misc_dve silu_done bc_hi sp_act sp_chain sp_done "
            "delta_ready dd_ready rep_done ffn_loaded eo_free b1_ready take_ready back_loaded "
            "combined out_stored act_chain").split()}

        def tiles_of(c):
            stage_a = [(13, "x0", "act"), (14, "x1", "act"), (15, "z0", "act"), (15, "z1", "act"),
                       (18, "bc0", "dve"), (19, "v0", "act")]
            if c < 0:
                return stage_a
            t = [(1, "bc1", "dve"), (2, "v1", "act")]
            if c >= 1:
                t += [(4, "outp", "dve")]
            if c + 1 < CHUNKS:
                t += stage_a
            if FIRST_FFN <= c < FIRST_FFN + EXP:
                t += [(5, "xt0", "dve"), (6, "xt1", "dve"), (12, "o0", "dve"), (26, "o1", "dve")]
                t += [(7 + f, f"h0{f}", "act") for f in range(FT)]
                t += [(21 + f, f"h1{f}", "act") for f in range(FT)]
            return sorted(t, key=lambda x: x[0])

        base = {"misc_pe": [0], "misc_act": [0], "misc_dve": [0]}
        for c in range(-1, CHUNKS + 1):
            plan = tiles_of(c) if c < CHUNKS else []
            base["misc_pe"].append(base["misc_pe"][-1] + len(plan))
            for e in ("act", "dve"):
                base["misc_" + e].append(base["misc_" + e][-1] + sum(x[2] == e for x in plan))

        def lin(ch, of):
            first, it = ch
            v = of(first)
            return v if it is None else it * (of(first + 2) - v) + v

        def per_chunk(ch, n, k):
            return lin(ch, lambda c: n * c + k)

        def misc_count(ch, name, k=0):
            return lin(ch, lambda c: base[name][c + 1] + k)

        def tile_index(ch, name):
            return [x[1] for x in tiles_of(ch[0])].index(name)

        def tile_bank(ch, name):
            return misc[(base["misc_pe"][ch[0] + 1] + tile_index(ch, name)) % 2]

        def tile_made(ch, name):
            return misc_count(ch, "misc_pe", tile_index(ch, name) + 1)

        def tile_read(ch, name):
            plan = tiles_of(ch[0])
            n = tile_index(ch, name)
            eng = plan[n][2]
            return S["misc_" + eng], misc_count(ch, "misc_" + eng, sum(x[2] == eng for x in plan[:n + 1]))

        def wait(eng, name, value):
            if not isinstance(value, int) or value > 0:
                eng.wait_ge(S[name] if isinstance(name, str) else name, value)

        def chunks(eng, body, last, after_first=None):
            body((0, None))
            if after_first:
                after_first()
            with eng.Fori(0, EXP // 2) as it:
                body((FIRST_FFN, it))
                body((FIRST_FFN + 1, it))
            with eng.Fori(0, (CHUNKS - 1 - FIRST_COMBINE) // 2) as it:
                body((FIRST_COMBINE, it))
                body((FIRST_COMBINE + 1, it))
            body((CHUNKS - 1, None))
            last()

        def has(ch, name):
            return name in [x[1] for x in tiles_of(ch[0])]

        def has_ffn(ch):
            return FIRST_FFN <= ch[0] < FIRST_FFN + EXP

        def has_combine(ch):
            return ch[0] >= FIRST_COMBINE

        def after(ch):
            return (ch[0] + 1, ch[1])

        def before(ch):
            return (ch[0] - 1, ch[1])

        def xs_of(ch, hf):
            return xs[:, ch[0] % 2, hf, :]

        def zs_of(ch, hf):
            return zs[:, ch[0] % 2, hf, :]

        def head_of(w):
            return w % 2

        def sel_of(w, kind):
            u = w % UNITS
            return sel[:, kind * 16 + head_of(u) * 8 + u // 2, :, :].rearrange("k a d -> k (a d)")

        def steps(ap):
            return ap.rearrange("p (s t) -> p s t", s=SEQS)[:, :, 1:SEQ]

        block = ctx.enter_context(nc.Block())

        @block.sync
        def _(sp):
            sp.dma_start(con[:, :], consts[:, 0:K_COLS]).then_inc(S["con_loaded"], 16)
            for b in range(LN_BLK):
                sp.dma_start(acc[:, b * BT:(b + 1) * BT, :],
                             hidden[b * BT * P:(b + 1) * BT * P, :].rearrange("(i p) d -> p i d", p=P)
                             ).then_inc(S[f"x_loaded{b}"], 16)
            sp.dma_start(p_sb[:, 2:4, :].rearrange("p r t -> p (r t)"), consts[:, K_KEEP:K_ALL]
                         ).then_inc(S["con_loaded"], 16)
            sp.dma_start(r_con, consts[:, K_TRI:K_KEEP]).then_inc(S["con_loaded"], 16)
            sp.wait_ge(S["zero_ready"], 1)
            for b in range(EXP):
                sp.dma_start(ein[b * CAP:(b + 1) * CAP, :].rearrange("(i p) d -> p i d", p=P),
                             zero.unsqueeze(1).broadcast_to([P, CAP // P, DM])
                             ).then_inc(S["ein_zeroed"], 16)

            def replicate(ch, hf):
                sp.wait_ge(S["dd_ready"], per_chunk(ch, 2, hf + 1))
                for hh in range(2):
                    for n2 in range(2):
                        sp.dma_start(drep[n2 * HD:(n2 + 1) * HD, hf, hh, :, :],
                                     dd[hh * HD:(hh + 1) * HD, :, :]).then_inc(S["rep_done"], 16)

            replicate((0, None), 0)

            def body(ch):
                if has_ffn(ch):
                    sp.wait_ge(S["misc_dve"], misc_count(ch, "misc_dve"))
                    sp.wait_ge(S["scattered"], 16 * TILES)
                    sp.dma_start(xe, ein[bass.ds(lin(ch, lambda c: (c - FIRST_FFN) * CAP), CAP), :]
                                 .rearrange("(i p) d -> p i d", p=P)).then_inc(S["ffn_loaded"], 16)
                    sp.dma_start(w1_sb, w1[bass.ds(lin(ch, lambda c: (c - FIRST_FFN) * DM), DM), :]
                                 ).then_inc(S["ffn_loaded"], 16)
                    sp.dma_start(w2_sb, w2[bass.ds(lin(ch, lambda c: (c - FIRST_FFN) * FF), FF), :]
                                 .rearrange("(f p) m -> p f m", p=P)).then_inc(S["ffn_loaded"], 16)
                replicate(ch, 1)

                def store_expert(th):
                    s, v = tile_read(ch, f"o{th}")
                    sp.wait_ge(s, v)
                    sp.wait_ge(S["scattered"], 16 * TILES)
                    row = lin(ch, lambda c: (c - FIRST_FFN) * CAP + th * CH)
                    sp.dma_start(eout[bass.ds(row, CH), :].rearrange("(i p) d -> p i d", p=P),
                                 eo[:, th, :, :]).then_inc(S["eo_free"], 16)

                if has_ffn(ch):
                    store_expert(0)
                if ch[0] + 1 < CHUNKS:
                    replicate(after(ch), 0)
                if has_ffn(ch):
                    store_expert(1)
                if has_combine(ch):
                    store_group(ch, 0)

            def store_group(ch, extra):
                k = lin(ch, lambda c: c - FIRST_COMBINE + extra)
                sp.wait_ge(S["combined"], lin(ch, lambda c: c - FIRST_COMBINE + extra + 1))
                sp.wait_ge(S["eo_free"], 16 + 32 * EXP)
                row = lin(ch, lambda c: (c - FIRST_COMBINE + extra) * GROUP * P)
                tile0 = lin(ch, lambda c: (c - FIRST_COMBINE + extra) * GROUP)
                sp.dma_start(out[bass.ds(row, GROUP * P), :].rearrange("(i p) d -> p i d", p=P),
                             acc[:, bass.ds(tile0, GROUP), :]).then_inc(S["out_stored"], 16)

            def last():
                store_group((CHUNKS - 1, None), 1)
                sp.wait_ge(S["out_stored"], 16 * (TILES // GROUP))

            def load_b2():
                sp.wait_ge(S["scattered"], 16 * TILES)
                sp.dma_start(b2_bc, b2.partition_broadcast(P)).then_inc(S["eo_free"], 16)

            chunks(sp, body, last, load_b2)

        @block.gpsimd
        def _(pool):
            pool.memset(zero, 0.0).then_inc(S["zero_ready"], 1)
            pool.memset(xin, 0.0).then_inc(S["xin_zeroed"], 1)
            pool.memset(xnT[:, :, 0:TAPS - 1], 0.0).then_inc(S["xin_zeroed"], 1)
            pool.memset(weff[:, :, :], 0.0).then_inc(S["xin_zeroed"], 1)
            pool.memset(logc3, LOG_C[2]).then_inc(S["xin_zeroed"], 1)
            for b in range(LN_BLK):
                t = slice(b * BT, (b + 1) * BT)
                pool.wait_ge(S["ln_dve"], LN_BLK + 2 * b + 2)
                pool.tensor_tensor(xn[:, t, :], xn[:, t, :],
                                   rstd[:, t].unsqueeze(2).broadcast_to([P, BT, DM]),
                                   ALU.mult).then_inc(S["xn_ready"], 1)

            def softplus_end(ch, hf):
                pool.wait_ge(S["sp_done"], per_chunk(ch, 2, hf + 1))
                wait(pool, "rep_done", per_chunk(ch, 128, 64 * hf))
                if ch == (0, None) and hf == 0:
                    pool.wait_ge(S["ein_zeroed"], 16 * EXP)
                    pool.wait_ge(S["setup_pe"], 6)
                pool.tensor_tensor(dd[:, 0, :], sp_r[:, :], sp_l[:, :], ALU.add).then_inc(S["delta_ready"], 1)
                pool.wait_ge(S["delta_ready"], per_chunk(ch, 2, hf + 1))
                pool.tensor_tensor(dd[:, 1, :], dd[:, 0, :], xs_of(ch, hf), ALU.mult).then_inc(S["dd_ready"], 1)

            softplus_end((0, None), 0)

            def gathers(ch, extra=0):
                pool.wait_ge(S["eo_free"], 16 + 32 * EXP)
                for n in range(GROUP):
                    pool.indirect_dma_start(back[:, n, :], None, eout[:, :],
                                            bass.IndirectOffsetOnAxis(ap=take_now[:, n:n + 1], axis=0),
                                            ).then_inc(S["back_loaded"], 16)

            def body(ch):
                for w in range(SLOTS):
                    hf, hh = w // UNITS, head_of(w)
                    if w % UNITS == 0:
                        pool.wait_ge(S["rep_done"], per_chunk(ch, 128, 64 * (hf + 1)))
                    if w == 2 and has_combine(ch):
                        pool.wait_ge(S["take_ready"], lin(ch, lambda c: c - FIRST_COMBINE + 1))
                    pool.wait_ge(S["b_copied"], per_chunk(ch, SLOTS, w + 1))
                    pool.tensor_tensor(u_sb[:, w % RING, :], drep[:, hf, hh, 1, :], b_sb[:, w % RING, :],
                                       ALU.mult).then_inc(S["u_ready"], 1)
                    if ch[0] == 0:
                        if w == 0:
                            pool.wait_ge(S["routed"], 2)
                        for i in range(w * TILES // SLOTS, (w + 1) * TILES // SLOTS):
                            pool.indirect_dma_start(ein[:, :],
                                                    bass.IndirectOffsetOnAxis(ap=put_at[:, i:i + 1], axis=0),
                                                    xn[:, i, :], None).then_inc(S["scattered"], 16)
                    if w == 9:
                        softplus_end(ch, 1)
                    if w == 26 and ch[0] + 1 < CHUNKS:
                        softplus_end(after(ch), 0)
                    if w == 2 and has_combine(ch):
                        gathers(ch)

            def last():
                pool.wait_ge(S["take_ready"], TILES // GROUP)
                gathers((CHUNKS - 1, None), 1)

            chunks(pool, body, last)

        @block.scalar
        def _(act):
            act.preload_act_table_set("natural_log_exp_and_others")

            def load(dst, src):
                act.dma_start(dst, src).then_inc(S["w_loaded"], 16)

            with nc.allow_non_contiguous_dma("small weights"):
                load(w_nat[:, 0:4, :], in_w.rearrange("(a p) m -> p a m", p=P))
                load(cw, conv_w.rearrange("(h p) k -> p h k", p=P))
                load(wo_nat, out_w)
                load(dt_nat, dt_w.rearrange("(h p) r -> p h r", p=P))
                load(b1_nat, b1.rearrange("e (f p) -> (e f) p", p=P))
                load(x_dt, xp_w.rearrange("(h o) d -> o h d", h=HEADS)[0:RANK, :, :])
                load(wg_sb[:, :], wg)
                load(cb, conv_b.rearrange("(h p) -> p h", p=P))
                load(dtb, dt_b.rearrange("(h p) -> p h", p=P))
                load(dsk, d_skip.rearrange("(h p) -> p h", p=P))
                for n2 in range(2):
                    for h in range(HEADS):
                        load(a_neg[n2 * HD:(n2 + 1) * HD, h, :],
                             a_log[h * HD:(h + 1) * HD, :].rearrange("d (j b) -> d j b", b=2)[:, :, n2])
                act.wait_ge(S["xin_zeroed"], 4)
                for hf in range(HALVES):
                    for copy in range(2):
                        for kind in range(2):
                            for hh in range(2):
                                r0 = copy * 64 + kind * 32 + hh * 16
                                s0 = (hf * 2 + hh) * (RANK + 2 * NS) + RANK + kind * NS
                                act.dma_start(xin[r0:r0 + NS, hf, hh * HD:(hh + 1) * HD],
                                              xp_w[s0:s0 + NS, :]).then_inc(S["xin_loaded"], 16)
            act.wait_ge(S["w_loaded"], 16 * W_LOADS)
            act.activation(a_neg[:, :, :], a_neg[:, :, :], ACT.Exp).then_inc(S["a_ready"], 1)

            def square(b):
                act.wait_ge(S["ln_dve"], b + 1)
                if b >= 2:
                    act.wait_ge(S["ln_dve"], LN_BLK + 2 * (b - 2) + 1)
                act.activation(squares[b % 2].rearrange("p r (a d) -> p (r a) d", d=DM),
                               xn[:, b * BT:(b + 1) * BT, :], ACT.Square).then_inc(S["ln_act"], 1)

            def rsqrt(b):
                t = slice(b * BT, (b + 1) * BT)
                act.wait_ge(S["ln_dve"], LN_BLK + 2 * b + 1)
                act.activation(ln_t[:, t], var[:, t], ACT.Ln).then_inc(S["act_chain"], 1)
                act.wait_ge(S["act_chain"], b + 1)
                act.activation(rstd[:, t], ln_t[:, t], ACT.Exp, scale=-0.5).then_inc(S["route_act"], 1)

            square(0)
            square(1)
            def evac(dst, src, made):
                act.wait_ge(S["setup_pe"], made)
                act.activation(dst, src, ACT.Copy).then_inc(S["setup_act"], 1)

            for hf in range(HALVES):
                evac(wx[:, hf, :, :].rearrange("p k m -> p (k m)"), c_ps[hf][:, :], 1 + hf)
            evac(wzo[:, :, :].rearrange("p k m -> p (k m)"), y_ps[:, :], 3)
            evac(bcw[:, :, :].rearrange("p k m -> p (k m)"), b_ps[:, 0:2 * P], 4)
            evac(dtT.rearrange("p h d -> p (h d)"), b_ps[0:RANK, 256:512], 4)
            evac(b1c[:, :], misc[0][:, 0:EXP * FT], 5)
            for hh in range(2):
                r = slice(hh * HD, (hh + 1) * HD)
                evac(weff[r, :, hh * HD:(hh + 1) * HD],
                     misc[1][r, 0:2 * HD].rearrange("p (h d) -> p h d", h=2), 6)
            rsqrt(0)
            square(2)
            rsqrt(1)
            square(3)
            rsqrt(2)
            rsqrt(3)
            for j in range(CHUNKS):
                act.wait_ge(S["xnT_pe"], j + 1)
                act.activation(xnT[:, SEQS * j:SEQS * (j + 1), TAPS - 1:ROW],
                               misc[j % 2][:, :].rearrange("p (s t) -> p s t", s=SEQS),
                               ACT.Copy).then_inc(S["xnT_act"], 1)
            act.wait_ge(S["route_dve"], 1)
            act.activation(rt_b, rt_a, ACT.Exp).then_inc(S["route_act"], 1)

            def silus(ch, src):
                for n, name in enumerate(("x0", "x1", "z0", "z1")):
                    act.wait_ge(S["misc_pe"], tile_made(src, name))
                    hf = n % 2
                    dst = (xs_of if n < 2 else zs_of)(ch, hf)
                    bias = cb[:, hf:hf + 1] if n < 2 else 0.0
                    if n == 0:
                        wait(act, "g_ready", per_chunk(ch, 2, -2))
                    act.activation(dst, tile_bank(src, name)[:, :], ACT.Silu, bias=bias
                                   ).then_inc(S["misc_act"], 1)
                act.preload_act_table_set("natural_log_exp_and_others")

            def bc_high(ch, hf, src):
                act.wait_ge(S["misc_pe"], tile_made(src, f"bc{hf}"))
                act.activation(bc[:, hf, :], tile_bank(src, f"bc{hf}")[:, :], ACT.Copy).then_inc(S["bc_hi"], 1)

            def softplus_start(ch, hf, src):
                name = f"v{hf}"
                v = tile_bank(src, name)[:, :]
                act.wait_ge(S["misc_pe"], tile_made(src, name))
                wait(act, "delta_ready", per_chunk(ch, 2, hf))
                n = lambda k: per_chunk(ch, 6, 3 * hf + k)
                act.activation(sp_e[:, :], v, ACT.Abs, bias=dtb[:, hf:hf + 1]).then_inc(S["sp_act"], 1)
                act.activation(sp_r[:, :], v, ACT.Relu, bias=dtb[:, hf:hf + 1]).then_inc(S["misc_act"], 1)
                act.wait_ge(S["sp_act"], n(1))
                act.activation(sp_e[:, :], sp_e[:, :], ACT.Exp, scale=-1.0).then_inc(S["sp_act"], 1)
                act.wait_ge(S["sp_act"], n(2))
                act.activation(sp_l[:, :], sp_e[:, :], ACT.Ln, bias=1.0).then_inc(S["act_chain"], 1)
                act.activation(sp_q[:, :], sp_e[:, :], ACT.Identity, bias=logc3, scale=LOG_C[3]
                               ).then_inc(S["sp_act"], 1)

            def copy_b(ch, w):
                act.wait_ge(S["b_bcast"], per_chunk(ch, SLOTS, w + 1))
                act.activation(b_sb[:, w % RING, :], b_ps[:, :], ACT.Copy).then_inc(S["b_copied"], 1)

            def relu(ch, th, f):
                name = f"h{th}{f}"
                act.wait_ge(S["misc_pe"], tile_made(ch, name))
                act.activation(hT[:, f, :], tile_bank(ch, name)[:, :], ACT.Relu,
                               bias=b1_now[:, f:f + 1]).then_inc(S["misc_act"], 1)

            first = (0, None)
            start = (-1, None)
            silus(first, start)
            bc_high(first, 0, start)
            softplus_start(first, 0, start)
            copy_b(first, 0)

            def body(ch):
                for w in range(SLOTS):
                    hf, hh, j = w // UNITS, head_of(w), (w % UNITS) // 2
                    if w + 1 < SLOTS:
                        copy_b(ch, w + 1)
                    elif ch[0] + 1 < CHUNKS:
                        copy_b(after(ch), 0)
                    if w % UNITS == 0:
                        act.wait_ge(S["rep_done"], per_chunk(ch, 128, 64 * (hf + 1)))
                    if ch[0] == 0 and w < 2:
                        act.wait_ge(S["setup_dve"], 2)
                        act.wait_ge(S["a_ready"], 2)
                    else:
                        act.wait_ge(S["scan_done"], per_chunk(ch, SLOTS, w - 1))
                    act.activation(steps(decay[w % 2][:, :]), steps(drep[:, hf, hh, 0, :]), ACT.Exp,
                                   scale=a_neg[:, hf * 2 + hh, j:j + 1]).then_inc(S["decay_ready"], 1)
                    if w == 2:
                        bc_high(ch, 1, ch)
                    if w == 3:
                        softplus_start(ch, 1, ch)
                    if ch[0] + 1 < CHUNKS:
                        if w == 15:
                            silus(after(ch), ch)
                        if w == 19:
                            bc_high(after(ch), 0, ch)
                        if w == 20:
                            softplus_start(after(ch), 0, ch)
                    if has_ffn(ch):
                        for th, s0 in ((0, 8), (1, 22)):
                            if s0 <= w < s0 + FT:
                                relu(ch, th, w - s0)

            chunks(act, body, lambda: None)

        @block.vector
        def _(dve):
            for b in range(LN_BLK):
                t = slice(b * BT, (b + 1) * BT)
                dve.wait_ge(S[f"x_loaded{b}"], 16)
                dve.tensor_reduce(mean[:, t], acc[:, t, :], AX, ALU.add).then_inc(S["sp_chain"], 1)
                dve.wait_ge(S["sp_chain"], 2 * b + 1)
                dve.tensor_scalar(mean[:, t], mean[:, t], 1.0 / DM, None, ALU.mult).then_inc(S["sp_chain"], 1)
                dve.wait_ge(S["sp_chain"], 2 * b + 2)
                dve.tensor_tensor(xn[:, t, :], acc[:, t, :],
                                  mean[:, t].unsqueeze(2).broadcast_to([P, BT, DM]),
                                  ALU.subtract).then_inc(S["ln_dve"], 1)
                if b == 0:
                    dve.wait_ge(S["w_loaded"], 16 * W_LOADS)
                    for hf in range(HALVES):
                        for k in range(TAPS):
                            last = dve.tensor_scalar(wt[:, hf * TAPS + k, :], w_nat[:, hf, :],
                                                     cw[:, hf, k:k + 1], None, ALU.mult)
                    last.then_inc(S["setup_dve"], 1)
            n = 2 * LN_BLK
            for b in range(LN_BLK):
                t = slice(b * BT, (b + 1) * BT)
                dve.wait_ge(S["ln_act"], b + 1)
                dve.tensor_reduce(var[:, t], squares[b % 2].rearrange("p r (a d) -> p (r a) d", d=DM),
                                  AX, ALU.add).then_inc(S["sp_chain"], 1)
                n += 1
                dve.wait_ge(S["sp_chain"], n)
                dve.tensor_scalar(var[:, t], var[:, t], 1.0 / DM, EPS, ALU.mult, ALU.add).then_inc(S["ln_dve"], 1)
                dve.wait_ge(S["route_act"], b + 1)

                def link(ins):
                    nonlocal n
                    n += 1
                    ins.then_inc(S["sp_chain"], 1)
                    dve.wait_ge(S["sp_chain"], n)

                dve.wait_ge(S["ln_dve"], LN_BLK + 2 * b + 1)
                link(dve.tensor_tensor(ln_t[:, t], rstd[:, t], rstd[:, t], ALU.mult))
                link(dve.tensor_tensor(ln_t[:, t], ln_t[:, t], var[:, t], ALU.mult))
                link(dve.tensor_scalar(ln_t[:, t], ln_t[:, t], -0.5, 1.5, ALU.mult, ALU.add))
                dve.tensor_tensor(rstd[:, t], rstd[:, t], ln_t[:, t], ALU.mult).then_inc(S["ln_dve"], 1)
            dve.wait_ge(S["a_ready"], 1)
            dve.tensor_scalar(a_neg[:, :, :], a_neg[:, :, :], -1.0, None, ALU.mult).then_inc(S["a_ready"], 1)
            dve.wait_ge(S["con_loaded"], 16)
            i2 = con[:, K_I2:K_I2 + 64].rearrange("p (s a) -> p s a", a=2)
            dve.tensor_copy(sel[:, :, :, :], i2.unsqueeze(3).broadcast_to([P, 32, 2, HD])).then_inc(S["sp_chain"], 1)
            for d in decay:
                last = dve.memset(d[:, :].rearrange("p (s t) -> p s t", s=SEQS)[:, :, 0:1], 0.0)
            last.then_inc(S["setup_dve"], 1)
            n += 1

            by_e = lambda a: a.rearrange("p (i e) -> p i e", e=EXP)
            by_i = lambda a: a.rearrange("p (e i) -> p i e", e=EXP)
            over_e = lambda a: a.unsqueeze(2).broadcast_to([P, TILES, EXP])

            def link(ins):
                nonlocal n
                n += 1
                ins.then_inc(S["sp_chain"], 1)
                dve.wait_ge(S["sp_chain"], n)

            dve.wait_ge(S["logits_pe"], 1)
            dve.wait_ge(S["con_loaded"], 48)
            link(dve.tensor_reduce(r_max, by_e(y_ps[:, :]), AX, ALU.max))
            dve.tensor_tensor(by_e(rt_a), by_e(y_ps[:, :]), over_e(r_max), ALU.subtract).then_inc(S["route_dve"], 1)
            dve.wait_ge(S["route_act"], LN_BLK + 1)
            link(dve.tensor_reduce(r_sum, by_e(rt_b), AX, ALU.add))
            link(dve.reciprocal(r_sum, r_sum))
            link(dve.tensor_tensor(by_e(rt_b), by_e(rt_b), over_e(r_sum), ALU.mult))
            link(dve.tensor_reduce(r_max, by_e(rt_b), AX, ALU.max))
            link(dve.tensor_tensor(by_e(rt_a), by_e(rt_b), over_e(r_max), ALU.is_equal))
            link(dve.tensor_tensor(by_e(rt_a), by_e(rt_a),
                                   first_won.unsqueeze(1).broadcast_to([P, TILES, EXP]),
                                   ALU.mult))
            link(dve.tensor_reduce(r_t, by_e(rt_a), AX, ALU.max))
            dve.tensor_tensor(by_i(rt_hot), by_e(rt_a), over_e(r_t), ALU.is_equal).then_inc(S["route_dve"], 1)
            dve.wait_ge(S["route_pe"], 1)
            link(dve.tensor_copy(rt_tot, c_ps[1][:, :]))
            link(dve.tensor_tensor_scan(rt_pos, keep, rt_tot, 0.0, ALU.mult, ALU.add))
            link(dve.tensor_tensor(rt_pos, rt_pos, rt_tot, ALU.subtract))
            dve.tensor_tensor(rt_pos, c_ps[0][:, :], rt_pos, ALU.add).then_inc(S["route_dve"], 1)
            dve.wait_ge(S["route_dve"], 3)
            link(dve.scalar_tensor_tensor(rt_a, rt_pos, float(CAP), rt_hot, ALU.is_le, ALU.mult))
            link(dve.scalar_tensor_tensor(rt_pos, rt_pos, -1.0, first_row, ALU.add, ALU.add))
            link(dve.tensor_tensor(rt_pos, rt_pos, rt_a, ALU.mult))
            link(dve.tensor_reduce(r_slot, by_i(rt_pos), AX, ALU.add))
            link(dve.tensor_reduce(r_kept, by_i(rt_a), AX, ALU.add))
            dve.tensor_copy(take_at[:, :], r_slot).then_inc(S["routed"], 1)
            link(dve.tensor_tensor(gate, r_max, r_kept, ALU.mult))
            link(dve.tensor_scalar(r_t, r_kept, -1.0, 1.0, ALU.mult, ALU.add))
            link(dve.tensor_tensor(r_t, r_t, trash, ALU.mult))
            link(dve.tensor_tensor(r_t, r_t, r_slot, ALU.add))
            dve.tensor_copy(put_at[:, :], r_t).then_inc(S["routed"], 1)
            link0 = n

            def bc_low(ch, hf, src):
                t = tile_bank(src, f"bc{hf}")
                dve.wait_ge(S["bc_hi"], per_chunk(ch, 2, hf + 1))
                dve.tensor_tensor(bc[64:128, hf, :], t[64:128, :], bc_f[64:128, hf, :], ALU.subtract
                                  ).then_inc(S["misc_dve"], 1)

            def series(ch, hf, step):
                k = lambda s: per_chunk(ch, 8, 4 * hf + s + link0)
                if step == 0:
                    dve.wait_ge(S["sp_act"], per_chunk(ch, 6, 3 * hf + 3))
                    dve.tensor_tensor(sp_q[:, :], sp_q[:, :], sp_e[:, :], ALU.mult).then_inc(S["sp_chain"], 1)
                if step == 1:
                    dve.wait_ge(S["sp_chain"], k(1))
                    dve.scalar_tensor_tensor(sp_q[:, :], sp_q[:, :], LOG_C[1], sp_e[:, :], ALU.add, ALU.mult
                                             ).then_inc(S["sp_chain"], 1)
                    dve.tensor_scalar(sp_mask, sp_e[:, :], LOG_T, None, ALU.is_lt).then_inc(S["sp_chain"], 1)
                if step == 2:
                    dve.wait_ge(S["sp_chain"], k(3))
                    dve.scalar_tensor_tensor(sp_q[:, :], sp_q[:, :], LOG_C[0], sp_e[:, :], ALU.add, ALU.mult
                                             ).then_inc(S["sp_chain"], 1)
                if step == 3:
                    dve.copy_predicated(sp_l[:, :], sp_mask, sp_q[:, :]).then_inc(S["sp_done"], 1)

            def gate_half(ch, hf, step):
                if step == 0:
                    dve.wait_ge(S["sum_done"], per_chunk(ch, UNITS, UNITS // 2 * (hf + 1)))
                    dve.scalar_tensor_tensor(g_sb[:, hf, :], xs_of(ch, hf), dsk[:, hf:hf + 1], y_ps[:, :],
                                             ALU.mult, ALU.add).then_inc(S["y_read"], 1)
                else:
                    dve.wait_ge(S["y_read"], per_chunk(ch, 2, hf + 1))
                    dve.tensor_tensor(g_sb[:, hf, :], g_sb[:, hf, :], zs_of(ch, hf), ALU.mult
                                      ).then_inc(S["g_ready"], 1)

            def add_out(ch, src):
                bank_ = tile_bank(src, "outp") if src else misc[0]
                rows = acc[:, bass.ds(lin(ch, lambda c: c * CT), CT), :]
                dve.wait_ge(S["misc_pe"], tile_made(src, "outp") if src else base["misc_pe"][CHUNKS + 1] + 1)
                dve.tensor_tensor(rows, bank_[:, :].rearrange("p (i d) -> p i d", d=DM), rows, ALU.add
                                  ).then_inc(S["misc_dve"], 1)

            def expert_copy(ch, th):
                dve.wait_ge(S["misc_pe"], tile_made(ch, f"xt{th}"))
                dve.tensor_copy(xeT[:, th * CH:(th + 1) * CH], tile_bank(ch, f"xt{th}")[:, :]
                                ).then_inc(S["misc_dve"], 1)

            def expert_out(ch, th):
                dve.wait_ge(S["misc_pe"], tile_made(ch, f"o{th}"))
                dve.wait_ge(S["eo_free"], lin(ch, lambda c: 16 + 32 * (c - FIRST_FFN)))
                bias = b2_bc[:, bass.ds(lin(ch, lambda c: c - FIRST_FFN), 1), :]
                dve.tensor_tensor(eo[:, th, :, :], tile_bank(ch, f"o{th}")[:, :].rearrange("p (i d) -> p i d", d=DM),
                                  bias.broadcast_to([P, CT, DM]), ALU.add).then_inc(S["misc_dve"], 1)

            def take_indices(ch, extra=0):
                k = lin(ch, lambda c: (c - FIRST_COMBINE + extra) * GROUP)
                dve.tensor_copy(take_now[:, :], take_at[:, bass.ds(k, GROUP)]).then_inc(S["take_ready"], 1)

            def combine(ch, n, extra=0):
                dve.wait_ge(S["back_loaded"], lin(ch, lambda c: 16 * GROUP * (c - FIRST_COMBINE + extra + 1)))
                k = lin(ch, lambda c: (c - FIRST_COMBINE + extra) * GROUP + n)
                rows = acc[:, bass.ds(k, 1), :].rearrange("p i d -> p (i d)")
                return dve.scalar_tensor_tensor(rows, back[:, n, :], gate[:, bass.ds(k, 1)], rows,
                                                ALU.mult, ALU.add)

            first, start = (0, None), (-1, None)
            bc_low(first, 0, start)
            for s in range(4):
                if s == 3:
                    dve.wait_ge(S["sp_chain"], link0 + 4)
                series(first, 0, s)

            series_slots = (4, 5, 6, 8)

            def body(ch):
                for w in range(SLOTS):
                    hf = w // UNITS
                    wait(dve, "scan_done", per_chunk(ch, SLOTS, w))
                    dve.wait_ge(S["decay_ready"], per_chunk(ch, SLOTS, w + 1))
                    dve.wait_ge(S["u_ready"], per_chunk(ch, SLOTS, w + 1))
                    dve.tensor_tensor_scan(s_sb[:, w % RING, :], decay[w % 2][:, :], u_sb[:, w % RING, :], 0.0,
                                           ALU.mult, ALU.add).then_inc(S["scan_done"], 1)
                    if w > 0:
                        times_c(ch, w - 1)
                    elif ch[0] > 0:
                        times_c(before(ch), SLOTS - 1)
                    if w == 2 and ch[0] > 0:
                        gate_half(before(ch), 1, 0)
                    if w == 3 and ch[0] > 0:
                        gate_half(before(ch), 1, 1)
                    if w == UNITS + 2:
                        gate_half(ch, 0, 0)
                    if w == UNITS + 3:
                        gate_half(ch, 0, 1)
                    if w == 3:
                        bc_low(ch, 1, ch)
                    if w in series_slots:
                        series(ch, 1, series_slots.index(w))
                    if ch[0] + 1 < CHUNKS:
                        if w == 20:
                            bc_low(after(ch), 0, ch)
                        if w - 17 in series_slots:
                            series(after(ch), 0, series_slots.index(w - 17))
                    if w == 6 and ch[0] > 0:
                        add_out(before(ch), ch)
                    if has_ffn(ch):
                        if w == 5:
                            k = lin(ch, lambda c: (c - FIRST_FFN) * FT)
                            dve.tensor_copy(b1_now[:, :], b1c[:, bass.ds(k, FT)]).then_inc(S["b1_ready"], 1)
                        if w in (6, 7):
                            expert_copy(ch, w - 6)
                        if w == 13:
                            expert_out(ch, 0)
                        if w == 27:
                            expert_out(ch, 1)
                    if has_combine(ch):
                        if w == 0:
                            take_indices(ch)
                        if 20 <= w < 20 + GROUP:
                            ins = combine(ch, w - 20)
                            if w == 20 + GROUP - 1:
                                ins.then_inc(S["combined"], 1)

            def times_c(ch, w):
                dve.wait_ge(S["c_bcast"], per_chunk(ch, SLOTS, w + 1))
                dve.tensor_tensor(p_sb[:, w % RING, :], s_sb[:, w % RING, :], c_ps[w % 2][:, :], ALU.mult
                                  ).then_inc(S["p_ready"], 1)

            def last():
                end = (CHUNKS - 1, None)
                dve.wait_ge(S["scan_done"], SLOTS * CHUNKS)
                times_c(end, SLOTS - 1)
                take_indices(end, 1)
                gate_half(end, 1, 0)
                gate_half(end, 1, 1)
                add_out(end, None)
                dve.wait_ge(S["misc_dve"], base["misc_dve"][CHUNKS + 1] + 1)
                for k in range(GROUP):
                    ins = combine(end, k, 1)
                ins.then_inc(S["combined"], 1)

            chunks(dve, body, last)

        @block.tensor
        def _(pe):
            pe.wait_ge(S["con_loaded"], 16)
            pe.wait_ge(S["w_loaded"], 16 * W_LOADS)
            pe.wait_ge(S["setup_dve"], 1)
            for hf in range(HALVES):
                for k in range(TAPS):
                    mm = pe.transpose(c_ps[hf][:, k * P:(k + 1) * P], wt[:, hf * TAPS + k, :], ident)
                mm.then_inc(S["setup_pe"], 1)
            for k in range(4):
                src = w_nat[:, 2 + k, :] if k < 2 else wo_nat[:, (k - 2) * P:(k - 1) * P]
                mm = pe.transpose(y_ps[:, k * P:(k + 1) * P], src, ident)
            mm.then_inc(S["setup_pe"], 1)
            pe.wait_ge(S["xin_loaded"], 16 * 16)
            for hf in range(HALVES):
                pe.transpose(b_ps[:, hf * P:(hf + 1) * P], xin[:, hf, :], ident)
            for hf in range(HALVES):
                mm = pe.transpose(b_ps[0:RANK, 256 + hf * P:256 + (hf + 1) * P], dt_nat[:, hf, :], ident)
            mm.then_inc(S["setup_pe"], 1)
            pe.transpose(misc[0][:, 0:EXP * FT], b1_nat, con[0:EXP * FT, K_ID:K_ID + EXP * FT]
                         ).then_inc(S["setup_pe"], 1)
            pe.wait_ge(S["setup_act"], 5)
            for hf in range(HALVES):
                for hh in range(2):
                    h = hf * 2 + hh
                    mm = pe.matmul(misc[1][hh * HD:(hh + 1) * HD, hf * HD:(hf + 1) * HD], x_dt[:, h, :],
                                   dtT[:, hf, hh * HD:(hh + 1) * HD], start=True, stop=True)
            mm.then_inc(S["setup_pe"], 1)
            pe.wait_ge(S["setup_act"], 8)

            def logits(j):
                pe.wait_ge(S["xnT_act"], j + 1)
                for i in range(CT * j, CT * (j + 1)):
                    col = TAPS - 1 + P * (i % 2)
                    mm = pe.matmul(y_ps[:, i * EXP:(i + 1) * EXP], xnT[:, i // 2, col:col + P], wg_sb[:, :],
                                   start=True, stop=True)
                return mm

            for j in range(CHUNKS):
                pe.wait_ge(S["xn_ready"], j * CT // BT + 1)
                if j >= 2:
                    pe.wait_ge(S["xnT_act"], j - 1)
                for k in range(CT):
                    mm = pe.transpose(misc[j % 2][:, k * P:(k + 1) * P], xn[:, CT * j + k, :], ident)
                mm.then_inc(S["xnT_pe"], 1)
                if j >= 1:
                    logits(j - 1)
            logits(CHUNKS - 1).then_inc(S["logits_pe"], 1)

            def claim(src, name):
                plan = tiles_of(src[0])
                n = tile_index(src, name)
                if n >= 2:
                    pe.wait_ge(*tile_read(src, plan[n - 2][1]))
                elif n == 0 and src[0] >= 0:
                    pe.wait_ge(S["misc_act"], misc_count(src, "misc_act"))
                    pe.wait_ge(S["misc_dve"], misc_count(src, "misc_dve"))
                return tile_bank(src, name)

            def in_proj(ch, src, name):
                t = claim(src, name)
                hf = int(name[1])
                seqs = bass.ds(lin(ch, lambda c: c * SEQS), SEQS)
                if name[0] == "x":
                    for k in range(TAPS):
                        mm = pe.matmul(t[:, :], wx[:, hf, k, :], xnT[:, seqs, k:k + SEQ],
                                       start=(k == 0), stop=(k == TAPS - 1))
                else:
                    mm = pe.matmul(t[:, :], wz[:, hf, :], xnT[:, seqs, TAPS - 1:ROW], start=True, stop=True)
                mm.then_inc(S["misc_pe"], 1)

            def x_proj(ch, src, name):
                t = claim(src, name)
                hf = int(name[-1])
                if hf == 0:
                    pe.wait_ge(*tile_read(src, "x0"))
                w = bcw if name[0] == "b" else weff
                pe.matmul(t[:, :], w[:, hf, :], xs_of(ch, hf), start=True, stop=True).then_inc(S["misc_pe"], 1)

            def out_proj(ch, t):
                pe.wait_ge(S["g_ready"], per_chunk(ch, 2, 2))
                for i in range(CT):
                    for hf in range(HALVES):
                        mm = pe.matmul(t[:, i * P:(i + 1) * P], g_sb[:, hf, i * P:(i + 1) * P], wo[:, hf, :],
                                       start=(hf == 0), stop=(hf == HALVES - 1))
                mm.then_inc(S["misc_pe"], 1)

            def expert(ch, name):
                t = claim(ch, name)
                if name[:2] == "xt":
                    th = int(name[2])
                    if th == 0:
                        pe.wait_ge(S["ffn_loaded"], lin(ch, lambda c: 48 * (c - FIRST_FFN + 1)))
                    for k in range(CT):
                        mm = pe.transpose(t[:, k * P:(k + 1) * P], xe[:, th * CT + k, :], ident)
                elif name[0] == "h":
                    th, f = int(name[1]), int(name[2])
                    pe.wait_ge(*tile_read(ch, f"xt{th}"))
                    mm = pe.matmul(t[:, :], w1_sb[:, f * P:(f + 1) * P], xeT[:, th * CH:(th + 1) * CH],
                                   start=True, stop=True)
                else:
                    th = int(name[1])
                    pe.wait_ge(*tile_read(ch, f"h{th}{FT - 1}"))
                    for k in range(CT):
                        for f in range(FT):
                            mm = pe.matmul(t[:, k * P:(k + 1) * P], hT[:, f, k * P:(k + 1) * P], w2_sb[:, f, :],
                                           start=(f == 0), stop=(f == FT - 1))
                mm.then_inc(S["misc_pe"], 1)

            def bcast_b(ch, w):
                hf = w // UNITS
                if w % UNITS == 0:
                    pe.wait_ge(*tile_read(ch if hf else (before(ch) if ch[0] > 0 else (-1, None)), f"bc{hf}"))
                wait(pe, "b_copied", per_chunk(ch, SLOTS, w))
                pe.matmul(b_ps[:, :], sel_of(w, 0), bc[:, hf, :], start=True, stop=True).then_inc(S["b_bcast"], 1)

            def bcast_c(ch, w):
                wait(pe, "p_ready", per_chunk(ch, SLOTS, w - 1))
                pe.matmul(c_ps[w % 2][:, :], sel_of(w, 1), bc[:, w // UNITS, :], start=True, stop=True
                          ).then_inc(S["c_bcast"], 1)

            def sum_pair(ch, w):
                u = w % UNITS
                if u == 0:
                    wait(pe, "y_read", per_chunk(ch, 2, w // UNITS))
                pe.wait_ge(S["p_ready"], per_chunk(ch, SLOTS, w + 2))
                for hh in range(2):
                    mm = pe.matmul(y_ps[hh * HD:(hh + 1) * HD, :], con[:, K_I2:K_I2 + HD],
                                   p_sb[:, (w + hh) % RING, :], start=(u == 0), stop=(u == UNITS - 2))
                mm.then_inc(S["sum_done"], 1)

            first, start = (0, None), (-1, None)
            for name in ("x0", "x1", "z0", "z1"):
                if name == "x0":
                    pe.wait_ge(S["xnT_act"], CHUNKS)
                in_proj(first, start, name)
            x_proj(first, start, "bc0")
            x_proj(first, start, "v0")
            pe.wait_ge(S["route_dve"], 2)
            pe.matmul(c_ps[0][:, :], tri, rt_hot, start=True, stop=True)
            pe.matmul(c_ps[1][:, :], ones, rt_hot, start=True, stop=True).then_inc(S["route_pe"], 1)
            pe.wait_ge(S["setup_dve"], 2)
            bcast_b(first, 0)

            def body(ch):
                plan = tiles_of(ch[0])
                for w in range(SLOTS):
                    if w + 1 < SLOTS:
                        bcast_b(ch, w + 1)
                    elif ch[0] + 1 < CHUNKS:
                        bcast_b(after(ch), 0)
                    if ch[0] == 0 and w < 2:
                        pe.wait_ge(S["route_dve"], 3)
                    bcast_c(ch, w)
                    if w % 2:
                        if w >= 3:
                            sum_pair(ch, w - 3)
                        elif ch[0] > 0:
                            sum_pair(before(ch), SLOTS - 2)
                    for slot, name, _ in plan:
                        if slot != w:
                            continue
                        if name[0] in "xz" and name[1] in "01":
                            in_proj(after(ch), ch, name)
                        elif name[0] in "bv":
                            x_proj(ch if name[-1] == "1" else after(ch), ch, name)
                        elif name == "outp":
                            out_proj(before(ch), claim(ch, name))
                        else:
                            expert(ch, name)

            def last():
                end = (CHUNKS - 1, None)
                sum_pair(end, SLOTS - 2)
                pe.wait_ge(S["misc_act"], base["misc_act"][CHUNKS + 1])
                pe.wait_ge(S["misc_dve"], base["misc_dve"][CHUNKS + 1])
                out_proj(end, misc[0])

            chunks(pe, body, last)


_INS = ["L0_attn_hidden_states", "L0_attn_in_proj_w", "L0_attn_conv_w", "L0_attn_conv_b",
        "L0_attn_x_proj_w", "L0_attn_dt_proj_w", "L0_attn_dt_proj_b", "L0_attn_A_log", "L0_attn_Dskip",
        "L0_attn_out_proj_w", "L0_ffn_Wg", "L0_ffn_W1", "L0_ffn_b1", "L0_ffn_W2", "L0_ffn_b2"]


def _constants(np):
    c = np.zeros((P, K_ALL), np.float32)
    k = np.arange(P)
    c[:, K_ID:K_ID + P] = np.eye(P)
    c[:, K_TRI:K_TRI + P] = k[:, None] <= k[None, :]
    c[:, K_I2:K_I2 + 64] = (k[:, None] % 64) == np.arange(64)[None, :]
    col = np.arange(EXP * TILES)
    c[:, K_KEEP:K_KEEP + EXP * TILES] = col % TILES != 0
    c[:, K_BASE:K_ALL] = col // TILES * CAP
    c[:, K_FIRST:K_FIRST + EXP] = EXP - np.arange(EXP)
    c[:, K_TRASH:K_TRASH + TILES] = TOK + np.arange(TILES)[None, :] * P + k[:, None]
    c[:, K_ONE:K_ONE + P] = 1.0
    return c


def kernel(**inputs):
    import numpy as np
    import concourse.bacc as bacc
    from concourse.bass_utils import run_bass_kernel_spmd

    nc = bacc.Bacc("TRN2", target_bir_lowering=False, num_devices=1)
    flat = {"L0_attn_hidden_states": (TOK, DM), "L0_attn_conv_w": (DIN, TAPS),
            "L0_ffn_W1": (EXP * DM, FF), "L0_ffn_W2": (EXP * FF, DM)}
    arrays, args = {}, []
    for name in _INS + ["consts"]:
        a = _constants(np) if name == "consts" else np.ascontiguousarray(inputs[name])
        a = a.reshape(flat.get(name, a.shape))
        arrays[name] = a
        args.append(nc.dram_tensor(name, a.shape, mybir.dt.from_np(a.dtype), kind="ExternalInput").ap())
    out = nc.dram_tensor("out", (TOK, DM), F32, kind="ExternalOutput").ap()
    bass_mamba_moe(nc, *args, out)
    r = run_bass_kernel_spmd(nc, [arrays], core_ids=[0])
    return r.results[0]["out"].reshape(BATCH, SEQ, DM)
```

```python
import concourse.bass as bass
from concourse import mybir
from contextlib import ExitStack

F32 = mybir.dt.float32
F32R = mybir.dt.float32r
U32 = mybir.dt.uint32
ALU = mybir.AluOpType
ACT = mybir.ActivationFunctionType
AX = mybir.AxisListType.X

P = 128
BATCH, SEQ, DM = 32, 256, 128
TOK = BATCH * SEQ
TILES = TOK // P
DIN, HEADS, HD, NS, RANK, TAPS = 256, 4, 64, 16, 16, 4
HALVES = DIN // P
CH = 512
CHUNKS = TOK // CH
SEQS = CH // SEQ
CT = CH // P
ROW = SEQ + TAPS - 1
UC = P // NS
UNITS = P // UC
SLOTS = HALVES * UNITS
QUADS = P // 32
U_RING, S_RING = 4, 2 * QUADS
HELP, HELP_LAST = 3, 1
SUM = QUADS + 2
LAST_GATHER = 22
AHEAD = 2
EXP, FF = 8, 512
CAP = TOK // EXP
FT = FF // P
LN_BLK = 4
BT = TILES // LN_BLK
GROUP = 8
FIRST_FFN, FIRST_COMBINE = 1, 9
EPS = 1e-5
W_LOADS = 8 + NS
LOG_T = 1.0 / 16
LOG_ROOT, LOG_S, LOG_A, LOG_K = 1.6978107941861031, 0.47611282583342374, 0.05505341993227696, 0.5859629024895762
STAGE_A = {"z0": (1,), "x0": (1, 4, 5, 7), "bc0": (8,), "v0": (11,), "z1": (12,), "x1": (15, 16, 17, 17),
           "B0": (23,), "B1": (23,), "C0": (23,), "C1": (23,), "bc1": (25,), "v1": (26,)}
BC_1 = {"B2": (0,), "B3": (0,), "C2": (1,), "C3": (1,)}
OUT_PROJ = (9, 10)
FFN = {"xt0": (18,), "xt1": (19,), "h00": (20,), "h01": (20,), "h02": (21,), "h03": (23,),
       "o0": (24, 24, 25, 25), "h10": (26,), "h11": (26,), "h12": (27,), "h13": (27,),
       "o1": (29, 29, 30, 30)}
SOFTPLUS = {"act": (2, 3, 4, 5), "series": (5, 7, 8), "end": (8,), "zero": (9,), "low": (13,),
            "high": (13,)}
GATE = (5, 6)
GATHER, COMBINE = 1, 14
READ_ACT, READ_DVE = 2, 1
K_ID, K_SUM, K_TRI, K_ONE, K_FIRST, K_TRASH, K_I2, K_KEEP, K_BASE = (
    0, 128, 256, 384, 512, 520, 584, 648, 1160)
K_COLS = K_TRI
K_ALL = K_BASE + EXP * TILES


def bass_mamba_moe(nc, hidden, in_w, conv_w, conv_b, xp_w, dt_w, dt_b, a_log, d_skip, out_w,
                   wg, w1, b1, w2, b2, consts, out):
    ctx = ExitStack()
    with ctx:
        def sb(name, shape, dt=F32):
            return ctx.enter_context(nc.sbuf_tensor(name, shape, dt))

        def sem(name):
            return ctx.enter_context(nc.semaphore(name))

        ein = nc.dram_tensor("expert_in", [2 * TOK, DM], F32, kind="Internal").ap()
        eout = nc.dram_tensor("expert_out", [TOK, DM], F32, kind="Internal").ap()

        acc = sb("acc", [P, TILES, DM])
        xn_pool = sb("xn", [P, TILES * DM])
        xn = xn_pool[:, :].rearrange("p (i d) -> p i d", d=DM)
        xnT = sb("xnT", [P, BATCH, ROW])
        con = sb("con", [P, K_COLS])
        ident = con[:, K_ID:K_ID + P]
        sel_d = sb("sel_d", [P, HD // UC, NS, UC], F32R)
        sel_bc = sb("sel_bc", [P, HD, UC], F32R)
        wx = sb("wx", [P, HALVES, TAPS, P])
        wzo = sb("wzo", [P, 4, P])
        wz, wo = wzo[:, 0:2, :], wzo[:, 2:4, :]
        weff = sb("weff", [P, HALVES, P])
        bcw = sb("bcw", [P, HALVES, P])
        wg_sb = sb("wg_sb", [P, 32])
        b1c = sb("b1c", [P, EXP * FT])
        b1_now = sb("b1_now", [P, FT])
        small = sb("small", [P, 64])
        cw = small[:, 0:8].rearrange("p (h k) -> p h k", h=HALVES)
        cb, dtb, dsk = small[:, 8:10], small[:, 10:12], small[:, 12:14]
        log_a, log_k = small[:, 14:15], small[:, 15:16]
        a_neg = sb("a_neg", [P, SLOTS])
        spot = [0]

        def over_xn(n):
            spot[0] += n
            return xn_pool[:, spot[0] - n:spot[0]]

        w1_sb = over_xn(FF)
        w2_sb = over_xn(FT * DM).rearrange("p (f m) -> p f m", f=FT)
        xe = over_xn(CAP).rearrange("p (i d) -> p i d", d=DM)
        xeT = over_xn(CAP)
        hT = over_xn(FT * CH).rearrange("p (f t) -> p f t", f=FT)
        eo = over_xn(2 * CH).rearrange("p (h i d) -> p h i d", h=2, d=DM)
        back = over_xn(GROUP * DM).rearrange("p (i d) -> p i d", d=DM)
        b2_bc = over_xn(EXP * DM).rearrange("p (e d) -> p e d", d=DM)
        xs = sb("xs", [P, 2, HALVES, CH])
        zs = sb("zs", [P, 2, HALVES, CH])
        bc = sb("bc", [P, CH], F32R)
        bc_f = bc[:, :].bitcast(F32)
        sp_e, sp_q = [sb(f"sp_{n}", [P, CH])[:, :] for n in "eq"]
        hi = sb("hi", [P, 2, CH], F32R)[:, :, :]
        sp_r, sp_l = [sb(f"sp_{n}", [P, CH]) for n in "rl"]
        sp_m = sb("sp_m", [P, CH // 2])
        sp_mask = sp_m[:, :].bitcast(mybir.dt.uint16)
        dd_r = sb("dd", [P, 2, CH], F32R)
        dd, lo = dd_r[:, :, :].bitcast(F32), dd_r[:, :, :]
        dsp = sb("dsp", [P, HALVES, 2, 2, CH], F32R)
        b_of = sb("b_of", [P, HALVES, 2, CH])
        c_of = sb("c_of", [P, HALVES, 2, CH])
        u_sb = sb("u_sb", [P, U_RING, CH])
        s_sb = sb("s_sb", [P, S_RING, CH])
        g_sb = sb("g_sb", [P, HALVES, CH])
        w_nat = b_of[:, :, :, :].rearrange("p h r (a m) -> p (h r a) m", m=DM)
        wt = s_sb[:, 4:6, :].rearrange("p r (a m) -> p (r a) m", m=DM)
        wo_nat = s_sb[:, 0, 0:DIN]
        xin = s_sb[:, 0, DIN:DIN + 2 * P].rearrange("p (h d) -> p h d", h=2)
        dt_nat = s_sb[:, 1, 0:2 * RANK].rearrange("p (h r) -> p h r", h=2)
        b1_nat = s_sb[0:EXP * FT, 1, 32:32 + P]
        x_dt = s_sb[0:RANK, 1, 160:160 + HEADS * HD].rearrange("p (h d) -> p h d", h=HEADS)
        dtT = dd[0:RANK, 0, 0:DIN].rearrange("p (h d) -> p h d", h=HALVES)
        zero = dd[:, 1, 0:DM]
        squares = [u_sb[:, :, :], c_of[:, :, :, :].rearrange("p a b t -> p (a b) t")]
        ln = sp_m[:, 0:4 * TILES].rearrange("p (n i) -> p n i", n=4)
        mean, var, rstd, ln_t = (ln[:, n, :] for n in range(4))
        rt_a, rt_b = xs[:, 1, 0, :], xs[:, 1, 1, :]
        rt_hot, rt_pos = zs[:, 1, 0, :], zs[:, 1, 1, :]
        lt = zs[:, 1, :, :]
        rt_tot = g_sb[:, 0, :]
        r_con = g_sb[:, 1, 0:K_KEEP - K_TRI]
        tri, ones = r_con[:, 0:P], r_con[:, P:2 * P]
        first_won, trash = r_con[:, K_FIRST - K_TRI:K_TRASH - K_TRI], r_con[:, K_TRASH - K_TRI:K_I2 - K_TRI]
        keep, first_row = s_sb[:, 6, :], s_sb[:, 7, :]
        rt = s_sb[:, 2, 0:5 * TILES].rearrange("p (n i) -> p n i", n=5)
        r_max, r_sum, r_kept, r_slot, r_t = (rt[:, n, :] for n in range(5))
        gate = sb("gate", [P, TILES])[:, :]
        put_at = sb("put_at", [P, TILES], U32)
        take_at = sb("take_at", [P, TILES], U32)
        take_now = sb("take_now", [P, GROUP], U32)

        bank = [ctx.enter_context(nc.psum_tensor(f"bank{i}", [P, CH], F32)) for i in range(8)]
        decay = bank[0:3]
        du_ps = bank[3:5]
        y_ps = bank[5]
        misc = bank[6:8]
        lt_ps, lg_ps = decay[0:2], (decay[2], y_ps)

        S = {n: sem(n) for n in (
            "x_loaded0 x_loaded1 x_loaded2 x_loaded3 con_loaded w_loaded xin_zeroed xin_loaded "
            "setup_dve setup_pe setup_act a_ready zero_ready ein_zeroed "
            "ln_act xn_ready xnT_pe xnT_act logits_pe route_dve route_act route_pe routed "
            "centred_dve centred_pool log_chain var_ready rstd_ready xn_last lt_pe lt_act lg_read "
            "scattered du_spread delta_spread u_ready decay_ready scan_done p_dve p_ready sum_done "
            "y_read g_ready misc_pe misc_act misc_dve misc_low misc_copy bc_hi sp_act sp_chain sp_done "
            "delta_ready dx_ready dd_ready hi_ready lo_ready stacked ffn_loaded eo_free b1_ready take_ready back_loaded "
            "combined combine_last out_stored act_chain in_w_loaded").split()}

        def tiles_of(c):
            stage_a = [(STAGE_A[n], n, r) for n, r in (
                ("z0", "act"), ("x0", "act"), ("bc0", "low"), ("v0", "act"), ("z1", "act"), ("x1", "act"),
                ("B0", "copy"), ("B1", "copy"), ("C0", "copy"), ("C1", "copy"), ("bc1", "low"), ("v1", "act"))]
            if c < 0:
                return stage_a
            t = [(BC_1[n], n, "copy") for n in ("B2", "B3", "C2", "C3")]
            if c >= 1:
                t += [(OUT_PROJ, "outp", "dve")]
            if FIRST_FFN <= c < FIRST_FFN + EXP:
                t += [(FFN[n], n, "dve" if n[0] == "o" else "act") for n in FFN]
            if c + 1 < CHUNKS:
                t += stage_a
            return sorted(t, key=lambda x: x[0][0])

        def read_slot(plan, name):
            slots, _, by = next(x for x in plan if x[1] == name)
            return slots[-1] + (READ_ACT if by in ("act", "copy") else READ_DVE)

        def softplus_slots(hf):
            v = STAGE_A[f"v{hf}"][0]
            return {what: [v + k for k in after_v] for what, after_v in SOFTPLUS.items()}

        def softplus_now(ch, w, what):
            found = []
            for hf in range(HALVES):
                at = softplus_slots(hf)[what]
                for step, slot in enumerate(at):
                    if slot % SLOTS == w:
                        of = after(ch) if slot < SLOTS else ch
                        if of[0] < CHUNKS:
                            found.append((of, hf, step))
            return found

        def softplus_before(hf, what):
            at = softplus_slots(hf)[what]
            return [k for k, slot in enumerate(at) if slot < SLOTS]

        base = {"misc_pe": [0], "misc_act": [0], "misc_dve": [0], "misc_low": [0], "misc_copy": [0]}
        for c in range(-1, CHUNKS + 1):
            plan = tiles_of(c) if c < CHUNKS else []
            base["misc_pe"].append(base["misc_pe"][-1] + len(plan))
            for e in ("act", "dve", "low", "copy"):
                base["misc_" + e].append(base["misc_" + e][-1] + sum(x[2] == e for x in plan))

        def lin(ch, of):
            first, it = ch
            v = of(first)
            return v if it is None else it * (of(first + 2) - v) + v

        def per_chunk(ch, n, k):
            return lin(ch, lambda c: n * c + k)

        def misc_count(ch, name, k=0):
            return lin(ch, lambda c: base[name][c + 1] + k)

        def tile_index(ch, name):
            return [x[1] for x in tiles_of(ch[0])].index(name)

        def tile_bank(ch, name):
            return misc[(base["misc_pe"][ch[0] + 1] + tile_index(ch, name)) % 2]

        def tile_made(ch, name):
            return misc_count(ch, "misc_pe", tile_index(ch, name) + 1)

        def tile_read(ch, name):
            plan = tiles_of(ch[0])
            n = tile_index(ch, name)
            eng = plan[n][2]
            return S["misc_" + eng], misc_count(ch, "misc_" + eng, sum(x[2] == eng for x in plan[:n + 1]))

        def wait(eng, name, value):
            if not isinstance(value, int) or value > 0:
                eng.wait_ge(S[name] if isinstance(name, str) else name, value)

        def chunks(eng, body, last, after_first=None):
            body((0, None))
            if after_first:
                after_first()
            with eng.Fori(0, EXP // 2) as it:
                body((FIRST_FFN, it))
                body((FIRST_FFN + 1, it))
            with eng.Fori(0, (CHUNKS - 1 - FIRST_COMBINE) // 2) as it:
                body((FIRST_COMBINE, it))
                body((FIRST_COMBINE + 1, it))
            body((CHUNKS - 1, None))
            last()

        def of_half(ch, hf, kind):
            return (ch if hf else before_or_start(ch)), f"{kind}{2 * hf + 1}"

        def before_or_start(ch):
            return before(ch) if ch[0] > 0 else (-1, None)

        def has_ffn(ch):
            return FIRST_FFN <= ch[0] < FIRST_FFN + EXP

        def has_combine(ch):
            return ch[0] >= FIRST_COMBINE

        def low_by_pool(ch):
            return has_ffn(ch)

        def after(ch):
            return (ch[0] + 1, ch[1])

        def before(ch):
            return (ch[0] - 1, ch[1])

        def xs_of(ch, hf):
            return xs[:, ch[0] % 2, hf, :]

        def zs_of(ch, hf):
            return zs[:, ch[0] % 2, hf, :]

        def head_of(w):
            return w % QUADS // 2

        def group_of(w):
            return w % 2 * QUADS + w % UNITS // QUADS

        def products(ch, units):
            dve = HELP * SLOTS // QUADS
            if ch[0] == 0 and ch[1] is None:
                return HELP * units // QUADS, units - HELP * units // QUADS
            if ch[0] == CHUNKS - 1:
                more = HELP_LAST * units // QUADS
                return dve + more, ch[0] * SLOTS + units - dve - more
            return dve, per_chunk(ch, SLOTS, units - dve)

        def by_dve(ch, w):
            return w % QUADS < {0: HELP, CHUNKS - 1: HELP_LAST}.get(ch[0], 0)

        def wait_products(eng, ch, units):
            of_dve, of_pool = products(ch, units)
            wait(eng, "p_dve", of_dve)
            wait(eng, "p_ready", of_pool)

        def centre(eng, b):
            t = slice(b * BT, (b + 1) * BT)
            return eng.tensor_tensor(xn[:, t, :], acc[:, t, :], mean[:, t].unsqueeze(2).broadcast_to([P, BT, DM]),
                                     ALU.subtract)

        def wait_centred(eng, b):
            eng.wait_ge(S["centred_pool" if b % 2 else "centred_dve"], b // 2 + 1)

        def decay_of(w):
            return decay[w % len(decay)]

        def steps(ap):
            return ap.rearrange("p (s t) -> p s t", s=SEQS)[:, :, 1:SEQ]

        block = ctx.enter_context(nc.Block())

        @block.sync
        def _(sp):
            sp.dma_start(con[:, :], consts[:, 0:K_COLS]).then_inc(S["con_loaded"], 16)

            def load_x(b):
                sp.dma_start(acc[:, b * BT:(b + 1) * BT, :],
                             hidden[b * BT * P:(b + 1) * BT * P, :].rearrange("(i p) d -> p i d", p=P)
                             ).then_inc(S[f"x_loaded{b}"], 16)

            def load(dst, src):
                sp.dma_start(dst, src).then_inc(S["w_loaded"], 16)

            load_x(0)
            load_x(1)
            sp.dma_start(w_nat[:, 0:4, :], in_w.rearrange("(a p) m -> p a m", p=P)).then_inc(S["in_w_loaded"], 16)
            with nc.allow_non_contiguous_dma("small weights"):
                sp.dma_start(cw, conv_w.rearrange("(h p) k -> p h k", p=P)).then_inc(S["in_w_loaded"], 16)
                load_x(2)
                load_x(3)
                load(wo_nat, out_w)
                load(dt_nat, dt_w.rearrange("(h p) r -> p h r", p=P))
                load(b1_nat, b1.rearrange("e (f p) -> (e f) p", p=P))
                load(x_dt, xp_w.rearrange("(h o) d -> o h d", h=HEADS)[0:RANK, :, :])
                load(wg_sb[:, 0:EXP], wg)
                load(cb, conv_b.rearrange("(h p) -> p h", p=P))
                load(dtb, dt_b.rearrange("(h p) -> p h", p=P))
                load(dsk, d_skip.rearrange("(h p) -> p h", p=P))
                sp.wait_ge(S["xin_zeroed"], 5)
                for hf in range(HALVES):
                    for copy in range(2):
                        for kind in range(2):
                            for hh in range(2):
                                r0 = copy * 64 + kind * 32 + hh * 16
                                s0 = (hf * 2 + hh) * (RANK + 2 * NS) + RANK + kind * NS
                                sp.dma_start(xin[r0:r0 + NS, hf, hh * HD:(hh + 1) * HD],
                                             xp_w[s0:s0 + NS, :]).then_inc(S["xin_loaded"], 16)
                for n in range(NS):
                    load(a_neg[n * UC:(n + 1) * UC, :], a_log.rearrange("(g d) n -> d n g", d=UC)[:, n, :])
            sp.dma_start(s_sb[:, 6:8, :].rearrange("p r t -> p (r t)"), consts[:, K_KEEP:K_ALL]
                         ).then_inc(S["con_loaded"], 16)
            sp.dma_start(r_con, consts[:, K_TRI:K_KEEP]).then_inc(S["con_loaded"], 16)
            sp.wait_ge(S["zero_ready"], 1)
            for b in range(EXP):
                sp.dma_start(ein[b * CAP:(b + 1) * CAP, :].rearrange("(i p) d -> p i d", p=P),
                             zero.unsqueeze(1).broadcast_to([P, CAP // P, DM])
                             ).then_inc(S["ein_zeroed"], 16)

            def stack(ch, hf):
                sp.wait_ge(S["lo_ready"], per_chunk(ch, 2, hf + 1))
                for hh in range(2):
                    for n, part in enumerate((hi, lo)):
                        sp.dma_start(dsp[n * HD:(n + 1) * HD, hf, hh, :, :].bitcast(F32),
                                     part[hh * HD:(hh + 1) * HD, :, :].bitcast(F32)).then_inc(S["stacked"], 16)

            stack((0, None), 0)

            def body(ch):
                if has_ffn(ch):
                    sp.wait_ge(S["misc_dve"], misc_count(ch, "misc_dve"))
                    sp.wait_ge(S["scattered"], 16 * TILES)
                    sp.dma_start(xe, ein[bass.ds(lin(ch, lambda c: (c - FIRST_FFN) * CAP), CAP), :]
                                 .rearrange("(i p) d -> p i d", p=P)).then_inc(S["ffn_loaded"], 16)
                    sp.dma_start(w1_sb, w1[bass.ds(lin(ch, lambda c: (c - FIRST_FFN) * DM), DM), :]
                                 ).then_inc(S["ffn_loaded"], 16)
                    sp.dma_start(w2_sb, w2[bass.ds(lin(ch, lambda c: (c - FIRST_FFN) * FF), FF), :]
                                 .rearrange("(f p) m -> p f m", p=P)).then_inc(S["ffn_loaded"], 16)
                stack(ch, 1)

                def store_expert(th):
                    s, v = tile_read(ch, f"o{th}")
                    sp.wait_ge(s, v)
                    sp.wait_ge(S["scattered"], 16 * TILES)
                    row = lin(ch, lambda c: (c - FIRST_FFN) * CAP + th * CH)
                    sp.dma_start(eout[bass.ds(row, CH), :].rearrange("(i p) d -> p i d", p=P),
                                 eo[:, th, :, :]).then_inc(S["eo_free"], 16)

                if has_ffn(ch):
                    store_expert(0)
                if ch[0] + 1 < CHUNKS:
                    stack(after(ch), 0)
                if has_ffn(ch):
                    store_expert(1)
                if has_combine(ch):
                    store_group(ch, 0)

            def store_group(ch, extra):
                k = lin(ch, lambda c: c - FIRST_COMBINE + extra)
                sp.wait_ge(S["combined"], lin(ch, lambda c: c - FIRST_COMBINE + extra + 1))
                sp.wait_ge(S["eo_free"], 16 + 32 * EXP)
                row = lin(ch, lambda c: (c - FIRST_COMBINE + extra) * GROUP * P)
                tile0 = lin(ch, lambda c: (c - FIRST_COMBINE + extra) * GROUP)
                sp.dma_start(out[bass.ds(row, GROUP * P), :].rearrange("(i p) d -> p i d", p=P),
                             acc[:, bass.ds(tile0, GROUP), :]).then_inc(S["out_stored"], 16)

            def last():
                store_group((CHUNKS - 1, None), 1)
                sp.wait_ge(S["out_stored"], 16 * (TILES // GROUP))

            def load_b2():
                sp.wait_ge(S["scattered"], 16 * TILES)
                sp.dma_start(b2_bc, b2.partition_broadcast(P)).then_inc(S["eo_free"], 16)

            chunks(sp, body, last, load_b2)

        @block.gpsimd
        def _(pool):
            pool.memset(zero, 0.0).then_inc(S["zero_ready"], 1)
            pool.memset(xin, 0.0).then_inc(S["xin_zeroed"], 1)
            pool.memset(xnT[:, :, 0:TAPS - 1], 0.0).then_inc(S["xin_zeroed"], 1)
            pool.memset(weff[:, :, :], 0.0).then_inc(S["xin_zeroed"], 1)
            pool.memset(wg_sb[:, EXP:32], 0.0).then_inc(S["xin_zeroed"], 1)
            pool.memset(log_a, LOG_A)
            pool.memset(log_k, -LOG_K).then_inc(S["xin_zeroed"], 1)
            for b in (1, 3):
                pool.wait_ge(S["sp_chain"], 2 * b + 2)
                pool.wait_ge(S[f"x_loaded{b}"], 16)
                centre(pool, b).then_inc(S["centred_pool"], 1)
            for b in range(LN_BLK - 1):
                t = slice(b * BT, (b + 1) * BT)
                pool.wait_ge(S["rstd_ready"], b + 1)
                pool.tensor_tensor(xn[:, t, :], xn[:, t, :],
                                   rstd[:, t].unsqueeze(2).broadcast_to([P, BT, DM]),
                                   ALU.mult).then_inc(S["xn_ready"], 1)

            def softplus_end(ch, hf):
                pool.wait_ge(S["sp_done"], per_chunk(ch, 2, hf + 1))
                wait(pool, "stacked", per_chunk(ch, 128, 64 * hf))
                if ch == (0, None) and hf == 0:
                    pool.wait_ge(S["ein_zeroed"], 16 * EXP)
                    pool.wait_ge(S["setup_pe"], 6)
                pool.tensor_tensor(dd[:, 0, :], sp_r[:, :], sp_l[:, :], ALU.add).then_inc(S["delta_ready"], 1)
                pool.wait_ge(S["delta_ready"], per_chunk(ch, 2, hf + 1))
                pool.tensor_tensor(dd[:, 1, :], dd[:, 0, :], xs_of(ch, hf), ALU.mult).then_inc(S["dx_ready"], 1)

            def zero_first():
                pool.memset(dd[:, 0, :].rearrange("p (s t) -> p s t", s=SEQS)[:, :, 0:1], 0.0
                            ).then_inc(S["dd_ready"], 1)

            def split_low(ch, hf):
                pool.wait_ge(S["hi_ready"], per_chunk(ch, 2, hf + 1))
                pool.tensor_tensor(lo, dd, hi.bitcast(F32), ALU.subtract).then_inc(S["lo_ready"], 1)

            softplus_end((0, None), 0)
            pool.wait_ge(S["dx_ready"], 1)
            zero_first()
            split_low((0, None), 0)

            def gathers(tiles=range(GROUP)):
                for n in tiles:
                    pool.indirect_dma_start(back[:, n, :], None, eout[:, :],
                                            bass.IndirectOffsetOnAxis(ap=take_now[:, n:n + 1], axis=0),
                                            ).then_inc(S["back_loaded"], 16)

            def body(ch):
                for w in range(SLOTS):
                    hf, hh = w // UNITS, head_of(w)
                    if w == 1 and has_combine(ch):
                        pool.wait_ge(S["eo_free"], 16 + 32 * EXP)
                        pool.wait_ge(S["take_ready"], lin(ch, lambda c: c - FIRST_COMBINE + 1))
                    span = QUADS if ch[0] == 0 else 1
                    due = lambda what: [x for v in range(w - span + 1, w + 1) if w % span == span - 1
                                        for x in softplus_now(ch, v, what)]
                    zero_now = due("zero")
                    for of, hf_, _ in zero_now:
                        pool.wait_ge(S["dx_ready"], per_chunk(of, 2, hf_ + 1))
                    if not by_dve(ch, w):
                        if not any(by_dve(ch, v) is False for v in range(w // UNITS * UNITS, w)):
                            pool.wait_ge(*tile_read(*of_half(ch, hf, "C")))
                        pool.wait_ge(S["scan_done"], per_chunk(ch, SLOTS, w + 1))
                        s_now = s_sb[:, w % S_RING, :]
                        pool.tensor_tensor(s_now, s_now, c_of[:, hf, hh, :], ALU.mult).then_inc(S["p_ready"], 1)
                    if zero_now:
                        zero_first()
                    if ch[0] == 0:
                        if w == 0:
                            pool.wait_ge(S["routed"], 2)
                        for i in range(w * TILES // SLOTS, (w + 1) * TILES // SLOTS):
                            pool.indirect_dma_start(ein[:, :],
                                                    bass.IndirectOffsetOnAxis(ap=put_at[:, i:i + 1], axis=0),
                                                    xn[:, i, :], None).then_inc(S["scattered"], 16)
                    for of, hf_, _ in softplus_now(ch, w, "end"):
                        softplus_end(of, hf_)
                    if low_by_pool(ch):
                        for of, hf_, _ in due("low"):
                            split_low(of, hf_)
                    if GATHER <= w < GATHER + GROUP and has_combine(ch):
                        gathers((w - GATHER,))
                    if ch[0] == CHUNKS - 1 and LAST_GATHER <= w < LAST_GATHER + GROUP:
                        if w == LAST_GATHER:
                            pool.wait_ge(S["take_ready"], TILES // GROUP)
                        gathers((w - LAST_GATHER,))

            chunks(pool, body, lambda: None)

        @block.scalar
        def _(act):
            act.preload_act_table_set("natural_log_exp_and_others")

            def square(b):
                wait_centred(act, b)
                if b >= 2:
                    act.wait_ge(S["var_ready"], b - 1)
                act.activation(squares[b % 2].rearrange("p r (a d) -> p (r a) d", d=DM),
                               xn[:, b * BT:(b + 1) * BT, :], ACT.Square).then_inc(S["ln_act"], 1)

            def rsqrt(b):
                t = slice(b * BT, (b + 1) * BT)
                act.wait_ge(S["var_ready"], b + 1)
                act.activation(ln_t[:, t], var[:, t], ACT.Ln).then_inc(S["act_chain"], 1)
                act.wait_ge(S["act_chain"], b + 1)
                act.activation(rstd[:, t], ln_t[:, t], ACT.Exp, scale=-0.5).then_inc(S["route_act"], 1)

            square(0)
            square(1)
            rsqrt(0)
            square(2)
            rsqrt(1)
            square(3)
            def evac(dst, src, made):
                act.wait_ge(S["setup_pe"], made)
                act.activation(dst, src, ACT.Copy).then_inc(S["setup_act"], 1)

            for hf in range(HALVES):
                evac(wx[:, hf, :, :].rearrange("p k m -> p (k m)"), du_ps[hf][:, :], 1 + hf)
            evac(wzo[:, :, :].rearrange("p k m -> p (k m)"), y_ps[:, :], 3)
            evac(bcw[:, :, :].rearrange("p k m -> p (k m)"), decay[2][:, 0:2 * P], 4)
            evac(dtT.rearrange("p h d -> p (h d)"), decay[2][0:RANK, 256:512], 4)
            evac(b1c[:, :], misc[0][:, 0:EXP * FT], 5)
            for hh in range(2):
                r = slice(hh * HD, (hh + 1) * HD)
                evac(weff[r, :, hh * HD:(hh + 1) * HD],
                     misc[1][r, 0:2 * HD].rearrange("p (h d) -> p h d", h=2), 6)
            rsqrt(2)
            rsqrt(3)
            act.wait_ge(S["w_loaded"], 16 * W_LOADS)
            act.activation(a_neg[:, :], a_neg[:, :], ACT.Exp).then_inc(S["a_ready"], 1)
            def copy_logits(q):
                act.wait_ge(S["lt_pe"], q + 1)
                if q >= 2:
                    act.wait_ge(S["logits_pe"], q - 1)
                act.activation(lt[:, q % 2, :], lt_ps[q % 2][:, :], ACT.Copy).then_inc(S["lt_act"], 1)

            for j in range(CHUNKS):
                act.wait_ge(S["xnT_pe"], j + 1)
                act.activation(xnT[:, SEQS * j:SEQS * (j + 1), TAPS - 1:ROW],
                               du_ps[j % 2][:, :].rearrange("p (s t) -> p s t", s=SEQS),
                               ACT.Copy).then_inc(S["xnT_act"], 1)
                if j % 4 == 2 and j > 4:
                    copy_logits(j // 4 - 1)
            copy_logits(CHUNKS // 4 - 1)
            act.wait_ge(S["lg_read"], TILES // 16)
            act.activation(rt_b, rt_a, ACT.Exp).then_inc(S["route_act"], 1)

            def silus(ch, hf, src):
                if hf == 0:
                    wait(act, "g_ready", per_chunk(ch, 2, -2))
                act.wait_ge(S["misc_pe"], tile_made(src, f"z{hf}"))
                act.activation(zs_of(ch, hf), tile_bank(src, f"z{hf}")[:, :], ACT.Silu).then_inc(S["misc_act"], 1)
                act.wait_ge(S["misc_pe"], tile_made(src, f"x{hf}"))
                act.activation(xs_of(ch, hf), tile_bank(src, f"x{hf}")[:, :], ACT.Silu, bias=cb[:, hf:hf + 1]
                               ).then_inc(S["misc_act"], 1)
                act.preload_act_table_set("natural_log_exp_and_others")

            def bc_high(ch, hf, src):
                act.wait_ge(S["misc_pe"], tile_made(src, f"bc{hf}"))
                act.activation(bc[:, :], tile_bank(src, f"bc{hf}")[:, :], ACT.Copy).then_inc(S["bc_hi"], 1)

            def softplus_start(ch, hf, src, step):
                n = lambda k: per_chunk(ch, 8, 4 * hf + k)
                if step == 0:
                    name = f"v{hf}"
                    v = tile_bank(src, name)[:, :]
                    act.wait_ge(S["misc_pe"], tile_made(src, name))
                    wait(act, "delta_ready", per_chunk(ch, 2, hf))
                    act.activation(sp_e, v, ACT.Abs, bias=dtb[:, hf:hf + 1]).then_inc(S["sp_act"], 1)
                    act.activation(sp_r[:, :], v, ACT.Relu, bias=dtb[:, hf:hf + 1]).then_inc(S["misc_act"], 1)
                if step == 1:
                    act.wait_ge(S["sp_act"], n(1))
                    act.activation(sp_e, sp_e, ACT.Exp, scale=-1.0).then_inc(S["sp_act"], 1)
                if step == 2:
                    act.wait_ge(S["sp_act"], n(2))
                    act.activation(sp_l[:, :], sp_e, ACT.Ln, bias=1.0).then_inc(S["act_chain"], 1)
                    act.activation(sp_q, sp_e, ACT.Square, bias=log_a, scale=LOG_S).then_inc(S["sp_act"], 1)
                if step == 3:
                    act.wait_ge(S["sp_act"], n(3))
                    act.activation(sp_q, sp_q, ACT.Identity, bias=log_k, scale=-1.0).then_inc(S["sp_act"], 1)

            def split_high(ch, hf):
                act.wait_ge(S["dd_ready"], per_chunk(ch, 2, hf + 1))
                act.activation(hi, dd, ACT.Copy).then_inc(S["hi_ready"], 1)

            def copy_bc(ch, src, kind, hf):
                if kind == "B":
                    wait(act, "u_ready", per_chunk(ch, SLOTS, UNITS * (hf - 1)))
                elif hf == 0 and ch[0] > 0:
                    wait_products(act, before(ch), UNITS)
                elif ch[0] > 0:
                    wait_products(act, ch, 0)
                for hh in range(2):
                    name = f"{kind}{2 * hf + hh}"
                    act.wait_ge(S["misc_pe"], tile_made(src, name))
                    act.activation((b_of if kind == "B" else c_of)[:, hf, hh, :], tile_bank(src, name)[:, :],
                                   ACT.Copy).then_inc(S["misc_copy"], 1)

            def expert_copy(ch, th):
                act.wait_ge(S["misc_pe"], tile_made(ch, f"xt{th}"))
                act.activation(xeT[:, th * CH:(th + 1) * CH], tile_bank(ch, f"xt{th}")[:, :], ACT.Copy
                               ).then_inc(S["misc_act"], 1)

            def relu(ch, th, f):
                name = f"h{th}{f}"
                act.wait_ge(S["misc_pe"], tile_made(ch, name))
                act.activation(hT[:, f, :], tile_bank(ch, name)[:, :], ACT.Relu,
                               bias=b1_now[:, f:f + 1]).then_inc(S["misc_act"], 1)

            first = (0, None)
            start = (-1, None)
            silus(first, 0, start)
            bc_high(first, 0, start)
            for step in softplus_before(0, "act"):
                softplus_start(first, 0, start, step)
            silus(first, 1, start)
            copy_bc(first, start, "B", 0)
            copy_bc(first, start, "C", 0)
            split_high(first, 0)
            bc_high(first, 1, start)
            for step in softplus_before(1, "act"):
                softplus_start(first, 1, start, step)

            def body(ch):
                plan = tiles_of(ch[0])
                for w in range(SLOTS):
                    if ch[0] == 0 and w == 0:
                        act.wait_ge(S["a_ready"], 2)
                    act.wait_ge(S["delta_spread"], per_chunk(ch, SLOTS, w + 1))
                    d = steps(decay_of(w)[:, :])
                    k = w // UNITS * UNITS + w % QUADS * QUADS + w % UNITS // QUADS
                    act.activation(d, d, ACT.Exp, scale=a_neg[:, k:k + 1]).then_inc(S["decay_ready"], 1)
                    for of, hf_, _ in softplus_now(ch, w, "high"):
                        split_high(of, hf_)
                    for of, hf_, step in softplus_now(ch, w, "act"):
                        if step > 0:
                            softplus_start(of, hf_, None, step)
                    for _, name, by in plan:
                        if by in ("dve",) or read_slot(plan, name) + (by == "low") != w:
                            continue
                        hf_ = int(name[-1])
                        if name in ("x0", "x1"):
                            silus(after(ch), hf_, ch)
                        elif by == "low":
                            bc_high(after(ch), hf_, ch)
                        elif name[0] == "v":
                            softplus_start(after(ch), hf_, ch, 0)
                        elif by == "copy" and hf_ % 2:
                            copy_bc(after(ch) if hf_ < 2 else ch, ch, name[0], hf_ // 2)
                        elif name[:2] == "xt":
                            expert_copy(ch, hf_)
                        elif name[0] == "h":
                            relu(ch, int(name[1]), int(name[2]))

            chunks(act, body, lambda: None)

        @block.vector
        def _(dve):
            for b in range(LN_BLK):
                t = slice(b * BT, (b + 1) * BT)
                dve.wait_ge(S[f"x_loaded{b}"], 16)
                dve.tensor_reduce(mean[:, t], acc[:, t, :], AX, ALU.add).then_inc(S["sp_chain"], 1)
                dve.wait_ge(S["sp_chain"], 2 * b + 1)
                dve.tensor_scalar(mean[:, t], mean[:, t], 1.0 / DM, None, ALU.mult).then_inc(S["sp_chain"], 1)
                if b % 2 == 0:
                    dve.wait_ge(S["sp_chain"], 2 * b + 2)
                    centre(dve, b).then_inc(S["centred_dve"], 1)
            n = 2 * LN_BLK

            def link(ins):
                nonlocal n
                n += 1
                ins.then_inc(S["sp_chain"], 1)
                dve.wait_ge(S["sp_chain"], n)

            def variance(b):
                t = slice(b * BT, (b + 1) * BT)
                dve.wait_ge(S["ln_act"], b + 1)
                link(dve.tensor_reduce(var[:, t], squares[b % 2].rearrange("p r (a d) -> p (r a) d", d=DM),
                                       AX, ALU.add))
                dve.tensor_scalar(var[:, t], var[:, t], 1.0 / DM, EPS, ALU.mult, ALU.add).then_inc(S["var_ready"], 1)

            def newton(b):
                t = slice(b * BT, (b + 1) * BT)
                dve.wait_ge(S["route_act"], b + 1)
                dve.wait_ge(S["var_ready"], b + 1)
                link(dve.tensor_tensor(ln_t[:, t], rstd[:, t], rstd[:, t], ALU.mult))
                link(dve.tensor_tensor(ln_t[:, t], ln_t[:, t], var[:, t], ALU.mult))
                link(dve.tensor_scalar(ln_t[:, t], ln_t[:, t], -0.5, 1.5, ALU.mult, ALU.add))
                dve.tensor_tensor(rstd[:, t], rstd[:, t], ln_t[:, t], ALU.mult).then_inc(S["rstd_ready"], 1)

            variance(0)
            variance(1)
            dve.wait_ge(S["in_w_loaded"], 32)
            for hf in range(HALVES):
                for k in range(TAPS):
                    ins = dve.tensor_scalar(wt[:, hf * TAPS + k, :], w_nat[:, hf, :],
                                            cw[:, hf, k:k + 1], None, ALU.mult)
            ins.then_inc(S["setup_dve"], 1)
            for b in range(LN_BLK):
                newton(b)
                if b + 2 < LN_BLK:
                    variance(b + 2)
            t = slice((LN_BLK - 1) * BT, TILES)
            dve.wait_ge(S["rstd_ready"], LN_BLK)
            dve.tensor_tensor(xn[:, t, :], xn[:, t, :], rstd[:, t].unsqueeze(2).broadcast_to([P, BT, DM]),
                              ALU.mult).then_inc(S["xn_last"], 1)
            dve.wait_ge(S["a_ready"], 1)
            dve.tensor_scalar(a_neg[:, :], a_neg[:, :], -1.0, None, ALU.mult).then_inc(S["a_ready"], 1)
            dve.wait_ge(S["con_loaded"], 48)
            i2 = r_con[:, K_I2 - K_TRI:K_I2 - K_TRI + HD]
            for g in range(HD // UC):
                dve.tensor_copy(sel_d[:, g, :, :],
                                i2[:, g * UC:(g + 1) * UC].unsqueeze(1).broadcast_to([P, NS, UC]))
            dve.tensor_copy(sel_bc[:, :, :], i2.unsqueeze(2).broadcast_to([P, HD, UC])).then_inc(S["sp_chain"], 1)
            n += 1

            def bc_low(ch, hf, src):
                t = tile_bank(src, f"bc{hf}")
                dve.wait_ge(S["bc_hi"], per_chunk(ch, 2, hf + 1))
                dve.tensor_tensor(bc[64:128, :], t[64:128, :], bc_f[64:128, :], ALU.subtract
                                  ).then_inc(S["misc_low"], 1)

            def series(ch, hf, step):
                k = lambda s: per_chunk(ch, 6, 3 * hf + s)
                if step == 0:
                    dve.wait_ge(S["sp_act"], per_chunk(ch, 8, 4 * hf + 4))
                    dve.tensor_tensor(sp_q, sp_q, sp_e, ALU.mult).then_inc(S["log_chain"], 1)
                if step == 1:
                    dve.tensor_scalar(sp_mask, sp_e, LOG_T, None, ALU.is_lt).then_inc(S["log_chain"], 1)
                    dve.wait_ge(S["log_chain"], k(1))
                    dve.scalar_tensor_tensor(sp_q, sp_e, -LOG_ROOT, sp_q, ALU.add, ALU.mult
                                             ).then_inc(S["log_chain"], 1)
                if step == 2:
                    dve.copy_predicated(sp_l[:, :], sp_mask, sp_q).then_inc(S["sp_done"], 1)

            def gate_half(ch, hf, step):
                if step == 0:
                    dve.wait_ge(S["sum_done"], per_chunk(ch, SLOTS // QUADS, UNITS // QUADS * (hf + 1)))
                    dve.scalar_tensor_tensor(g_sb[:, hf, :], xs_of(ch, hf), dsk[:, hf:hf + 1], y_ps[:, :],
                                             ALU.mult, ALU.add).then_inc(S["y_read"], 1)
                else:
                    dve.wait_ge(S["y_read"], per_chunk(ch, 2, hf + 1))
                    dve.tensor_tensor(g_sb[:, hf, :], g_sb[:, hf, :], zs_of(ch, hf), ALU.mult
                                      ).then_inc(S["g_ready"], 1)

            def add_out(ch, src, done=S["misc_dve"]):
                bank_ = tile_bank(src, "outp") if src else misc[0]
                rows = acc[:, bass.ds(lin(ch, lambda c: c * CT), CT), :]
                dve.wait_ge(S["misc_pe"], tile_made(src, "outp") if src else base["misc_pe"][CHUNKS + 1] + 1)
                dve.tensor_tensor(rows, bank_[:, :].rearrange("p (i d) -> p i d", d=DM), rows, ALU.add
                                  ).then_inc(done, 1)

            def expert_out(ch, th):
                dve.wait_ge(S["misc_pe"], tile_made(ch, f"o{th}"))
                dve.wait_ge(S["eo_free"], lin(ch, lambda c: 16 + 32 * (c - FIRST_FFN)))
                bias = b2_bc[:, bass.ds(lin(ch, lambda c: c - FIRST_FFN), 1), :]
                dve.tensor_tensor(eo[:, th, :, :], tile_bank(ch, f"o{th}")[:, :].rearrange("p (i d) -> p i d", d=DM),
                                  bias.broadcast_to([P, CT, DM]), ALU.add).then_inc(S["misc_dve"], 1)

            def take_indices(ch, extra=0):
                k = lin(ch, lambda c: (c - FIRST_COMBINE + extra) * GROUP)
                dve.tensor_copy(take_now[:, :], take_at[:, bass.ds(k, GROUP)]).then_inc(S["take_ready"], 1)

            def combine(ch, n, extra=0):
                dve.wait_ge(S["back_loaded"], lin(ch, lambda c: 16 * GROUP * (c - FIRST_COMBINE + extra + 1)))
                k = lin(ch, lambda c: (c - FIRST_COMBINE + extra) * GROUP + n)
                rows = acc[:, bass.ds(k, 1), :].rearrange("p i d -> p (i d)")
                return dve.scalar_tensor_tensor(rows, back[:, n, :], gate[:, bass.ds(k, 1)], rows,
                                                ALU.mult, ALU.add)

            def spread_u(ch, w):
                hf = w // UNITS
                if w % UNITS == 0:
                    dve.wait_ge(*tile_read(*of_half(ch, hf, "B")))
                dve.wait_ge(S["du_spread"], per_chunk(ch, SLOTS, w + 1))
                dve.tensor_tensor(u_sb[:, w % U_RING, :], du_ps[w % 2][:, :], b_of[:, hf, head_of(w), :], ALU.mult
                                  ).then_inc(S["u_ready"], 1)

            def split_low(ch, hf):
                dve.wait_ge(S["hi_ready"], per_chunk(ch, 2, hf + 1))
                dve.tensor_tensor(lo, dd, hi.bitcast(F32), ALU.subtract).then_inc(S["lo_ready"], 1)

            by_e = lambda a: a.rearrange("p (i e) -> p i e", e=EXP)
            by_i = lambda a: a.rearrange("p (e i) -> p i e", e=EXP)
            over_e = lambda a: a.unsqueeze(2).broadcast_to([P, TILES, EXP])

            dve.wait_ge(S["con_loaded"], 48)
            for q in range(TILES // 16):
                lg = lg_ps[q % 2][:, :].rearrange("p (k j c) -> p j k c", k=CT, j=4)[:, :, :, 0:EXP]
                m = r_max[:, 16 * q:16 * (q + 1)].rearrange("p (j k) -> p j k", k=CT)
                d = by_e(rt_a)[:, 16 * q:16 * (q + 1), :].rearrange("p (j k) e -> p j k e", k=CT)
                dve.wait_ge(S["logits_pe"], q + 1)
                link(dve.tensor_reduce(m, lg, AX, ALU.max))
                dve.tensor_tensor(d, lg, m.unsqueeze(3).broadcast_to([P, 4, CT, EXP]), ALU.subtract
                                  ).then_inc(S["lg_read"], 1)
            dve.wait_ge(S["route_act"], LN_BLK + 1)
            link(dve.tensor_reduce(r_sum, by_e(rt_b), AX, ALU.add))
            link(dve.reciprocal(r_sum, r_sum))
            link(dve.tensor_tensor(by_e(rt_b), by_e(rt_b), over_e(r_sum), ALU.mult))
            link(dve.tensor_reduce(r_max, by_e(rt_b), AX, ALU.max))
            link(dve.tensor_tensor(by_e(rt_a), by_e(rt_b), over_e(r_max), ALU.is_equal))
            link(dve.tensor_tensor(by_e(rt_a), by_e(rt_a),
                                   first_won.unsqueeze(1).broadcast_to([P, TILES, EXP]),
                                   ALU.mult))
            link(dve.tensor_reduce(r_t, by_e(rt_a), AX, ALU.max))
            dve.tensor_tensor(by_i(rt_hot), by_e(rt_a), over_e(r_t), ALU.is_equal).then_inc(S["route_dve"], 1)
            first, start = (0, None), (-1, None)
            bc_low(first, 0, start)
            for step in softplus_before(0, "series"):
                if step == 2:
                    dve.wait_ge(S["log_chain"], 3)
                series(first, 0, step)
            dve.wait_ge(S["route_pe"], 1)
            link(dve.tensor_copy(rt_tot, du_ps[1][:, :]))
            link(dve.tensor_tensor_scan(rt_pos, keep, rt_tot, 0.0, ALU.mult, ALU.add))
            link(dve.tensor_tensor(rt_pos, rt_pos, rt_tot, ALU.subtract))
            dve.tensor_tensor(rt_pos, du_ps[0][:, :], rt_pos, ALU.add).then_inc(S["route_dve"], 1)
            dve.wait_ge(S["route_dve"], 2)
            link(dve.scalar_tensor_tensor(rt_a, rt_pos, float(CAP), rt_hot, ALU.is_le, ALU.mult))
            link(dve.scalar_tensor_tensor(rt_pos, rt_pos, -1.0, first_row, ALU.add, ALU.add))
            link(dve.tensor_tensor(rt_pos, rt_pos, rt_a, ALU.mult))
            link(dve.tensor_reduce(r_slot, by_i(rt_pos), AX, ALU.add))
            link(dve.tensor_reduce(r_kept, by_i(rt_a), AX, ALU.add))
            dve.tensor_copy(take_at[:, :], r_slot).then_inc(S["routed"], 1)
            link(dve.tensor_tensor(gate, r_max, r_kept, ALU.mult))
            link(dve.tensor_scalar(r_t, r_kept, -1.0, 1.0, ALU.mult, ALU.add))
            link(dve.tensor_tensor(r_t, r_t, trash, ALU.mult))
            link(dve.tensor_tensor(r_t, r_t, r_slot, ALU.add))
            dve.tensor_copy(put_at[:, :], r_t).then_inc(S["routed"], 1)
            first, start = (0, None), (-1, None)
            bc_low(first, 1, start)
            for step in softplus_before(1, "series"):
                if step == 2:
                    dve.wait_ge(S["log_chain"], 6)
                series(first, 1, step)
            spread_u(first, 0)

            b1_slot = FFN["xt0"][0] - 2

            def body(ch):
                plan = tiles_of(ch[0])
                for w in range(SLOTS):
                    if w + 1 < SLOTS:
                        spread_u(ch, w + 1)
                    elif ch[0] + 1 < CHUNKS:
                        spread_u(after(ch), 0)
                    if w % QUADS == 0:
                        wait(dve, "sum_done", per_chunk(ch, SLOTS // QUADS, w // QUADS - 1))
                    for of, hf_, step in softplus_now(ch, w, "series"):
                        if step == 2:
                            dve.wait_ge(S["log_chain"], per_chunk(of, 6, 3 * (hf_ + 1)))
                    dve.wait_ge(S["decay_ready"], per_chunk(ch, SLOTS, w + 1))
                    dve.wait_ge(S["u_ready"], per_chunk(ch, SLOTS, w + 1))
                    dve.tensor_tensor_scan(s_sb[:, w % S_RING, :], decay_of(w)[:, :], u_sb[:, w % U_RING, :], 0.0,
                                           ALU.mult, ALU.add).then_inc(S["scan_done"], 1)
                    if w > 0 and by_dve(ch, w - 1):
                        if w - 1 in (0, UNITS):
                            dve.wait_ge(*tile_read(*of_half(ch, w // UNITS, "C")))
                        dve.wait_ge(S["scan_done"], per_chunk(ch, SLOTS, w))
                        s_now = s_sb[:, (w - 1) % S_RING, :]
                        dve.tensor_tensor(s_now, s_now, c_of[:, (w - 1) // UNITS, head_of(w - 1), :], ALU.mult
                                          ).then_inc(S["p_dve"], 1)
                    for step in range(2):
                        if w == GATE[step] and ch[0] > 0:
                            gate_half(before(ch), 1, step)
                        if w == UNITS + GATE[step]:
                            gate_half(ch, 0, step)
                    for of, hf_, step in softplus_now(ch, w, "series"):
                        series(of, hf_, step)
                    if not low_by_pool(ch):
                        for of, hf_, _ in softplus_now(ch, w, "low"):
                            split_low(of, hf_)
                    if has_ffn(ch) and w == b1_slot:
                        k = lin(ch, lambda c: (c - FIRST_FFN) * FT)
                        dve.tensor_copy(b1_now[:, :], b1c[:, bass.ds(k, FT)]).then_inc(S["b1_ready"], 1)
                    for _, name, by in plan:
                        if by not in ("dve", "low") or min(read_slot(plan, name) + (by == "low"), SLOTS - 1) != w:
                            continue
                        if by == "low":
                            bc_low(after(ch), int(name[2]), ch)
                        elif name == "outp":
                            add_out(before(ch), ch)
                        else:
                            expert_out(ch, int(name[1]))
                    if has_combine(ch):
                        if w == 0:
                            take_indices(ch)
                        if COMBINE <= w < COMBINE + GROUP:
                            ins = combine(ch, w - COMBINE)
                            if w == COMBINE + GROUP - 1:
                                ins.then_inc(S["combined"], 1)
                        if ch[0] == CHUNKS - 1 and w == min(COMBINE + GROUP, LAST_GATHER):
                            dve.wait_ge(S["combined"], TILES // GROUP - 1)
                            take_indices(ch, 1)

            def last():
                end = (CHUNKS - 1, None)
                for k in range(GROUP):
                    ins = combine(end, k, 1)
                ins.then_inc(S["combine_last"], 1)
                gate_half(end, 1, 0)
                gate_half(end, 1, 1)
                dve.wait_ge(S["combine_last"], 1)
                add_out(end, None, S["combined"])

            chunks(dve, body, last)

        @block.tensor
        def _(pe):
            pe.wait_ge(S["con_loaded"], 16)
            pe.wait_ge(S["w_loaded"], 16 * W_LOADS)
            pe.wait_ge(S["setup_dve"], 1)
            for hf in range(HALVES):
                for k in range(TAPS):
                    mm = pe.transpose(du_ps[hf][:, k * P:(k + 1) * P], wt[:, hf * TAPS + k, :], ident)
                mm.then_inc(S["setup_pe"], 1)
            for k in range(4):
                src = w_nat[:, 2 + k, :] if k < 2 else wo_nat[:, (k - 2) * P:(k - 1) * P]
                mm = pe.transpose(y_ps[:, k * P:(k + 1) * P], src, ident)
            mm.then_inc(S["setup_pe"], 1)
            pe.wait_ge(S["xin_loaded"], 16 * 16)
            for hf in range(HALVES):
                pe.transpose(decay[2][:, hf * P:(hf + 1) * P], xin[:, hf, :], ident)
            for hf in range(HALVES):
                mm = pe.transpose(decay[2][0:RANK, 256 + hf * P:256 + (hf + 1) * P], dt_nat[:, hf, :], ident)
            mm.then_inc(S["setup_pe"], 1)
            pe.transpose(misc[0][:, 0:EXP * FT], b1_nat, con[0:EXP * FT, K_ID:K_ID + EXP * FT]
                         ).then_inc(S["setup_pe"], 1)
            pe.wait_ge(S["setup_act"], 5)
            for hf in range(HALVES):
                for hh in range(2):
                    h = hf * 2 + hh
                    mm = pe.matmul(misc[1][hh * HD:(hh + 1) * HD, hf * HD:(hf + 1) * HD], x_dt[:, h, :],
                                   dtT[:, hf, hh * HD:(hh + 1) * HD], start=True, stop=True)
            mm.then_inc(S["setup_pe"], 1)
            pe.wait_ge(S["setup_act"], 8)

            def transposes(j):
                pe.wait_ge(S["xn_ready"], min(j * CT // BT + 1, LN_BLK - 1))
                if j * CT >= (LN_BLK - 1) * BT:
                    pe.wait_ge(S["xn_last"], 1)
                if j >= 2:
                    pe.wait_ge(S["xnT_act"], j - 1)
                for k in range(CT):
                    mm = pe.transpose(du_ps[j % 2][:, k * P:(k + 1) * P], xn[:, CT * j + k, :], ident)
                mm.then_inc(S["xnT_pe"], 1)

            def logits(q):
                pe.wait_ge(S["xnT_act"], 4 * (q + 1))
                if q >= 2:
                    pe.wait_ge(S["lt_act"], q - 1)
                for k in range(4):
                    j = 4 * q + k
                    mm = pe.matmul(lt_ps[q % 2][32 * k:32 * (k + 1), :], wg_sb[:, :],
                                   xnT[:, SEQS * j:SEQS * (j + 1), TAPS - 1:ROW], start=True, stop=True)
                mm.then_inc(S["lt_pe"], 1)

            def by_token(q):
                pe.wait_ge(S["lt_act"], q + 1)
                if q >= 2:
                    pe.wait_ge(S["lg_read"], q - 1)
                for k in range(CT):
                    mm = pe.transpose(lg_ps[q % 2][:, k * P:(k + 1) * P], lt[:, q % 2, k * P:(k + 1) * P], ident)
                mm.then_inc(S["logits_pe"], 1)

            for j in range(CHUNKS):
                transposes(j)
                if j % 4 == 1 and j > 4:
                    logits(j // 4 - 1)
                if j % 4 == 3 and j > 4:
                    by_token(j // 4 - 1)
            logits(CHUNKS // 4 - 1)
            by_token(CHUNKS // 4 - 1)

            def claim(src, name):
                plan = tiles_of(src[0])
                n = tile_index(src, name)
                if n >= 2:
                    pe.wait_ge(*tile_read(src, plan[n - 2][1]))
                elif n == 0 and src[0] >= 0:
                    pe.wait_ge(S["misc_act"], misc_count(src, "misc_act"))
                    pe.wait_ge(S["misc_dve"], misc_count(src, "misc_dve"))
                    pe.wait_ge(S["misc_low"], misc_count(src, "misc_low"))
                return tile_bank(src, name)

            def in_proj(ch, src, name, part):
                t = tile_bank(src, name) if part > 0 else claim(src, name)
                hf = int(name[1])
                seqs = bass.ds(lin(ch, lambda c: c * SEQS), SEQS)
                if name[0] == "x":
                    mm = pe.matmul(t[:, :], wx[:, hf, part, :], xnT[:, seqs, part:part + SEQ],
                                   start=(part == 0), stop=(part == TAPS - 1))
                else:
                    mm = pe.matmul(t[:, :], wz[:, hf, :], xnT[:, seqs, TAPS - 1:ROW], start=True, stop=True)
                if name[0] == "z" or part == TAPS - 1:
                    mm.then_inc(S["misc_pe"], 1)

            def x_proj(ch, src, name):
                t = claim(src, name)
                hf = int(name[-1])
                if name == "bc0":
                    pe.wait_ge(*tile_read(src, "x0"))
                elif name == "bc1":
                    pe.wait_ge(*tile_read(src, "x1"))
                w = bcw if name[0] == "b" else weff
                pe.matmul(t[:, :], w[:, hf, :], xs_of(ch, hf), start=True, stop=True).then_inc(S["misc_pe"], 1)

            def spread_bc(ch, src, name):
                h = int(name[1])
                pe.wait_ge(*tile_read(src if h < 2 else before_or_start(src), f"bc{h // 2}"))
                t = claim(src, name)
                k = ("BC".index(name[0]) * 2 + h % 2) * NS
                pe.matmul(t[:, :], sel_bc[:, k:k + NS, :].rearrange("k n d -> k (n d)"), bc[:, :],
                          start=True, stop=True).then_inc(S["misc_pe"], 1)

            def out_proj(ch, t, part):
                if part == 0:
                    pe.wait_ge(S["g_ready"], per_chunk(ch, 2, 2))
                for i in range(CT // 2 * part, CT // 2 * (part + 1)):
                    for hf in range(HALVES):
                        mm = pe.matmul(t[:, i * P:(i + 1) * P], g_sb[:, hf, i * P:(i + 1) * P], wo[:, hf, :],
                                       start=(hf == 0), stop=(hf == HALVES - 1))
                if part == 1:
                    mm.then_inc(S["misc_pe"], 1)

            def expert(ch, name, part):
                t = tile_bank(ch, name) if part > 0 else claim(ch, name)
                if name[:2] == "xt":
                    th = int(name[2])
                    if th == 0:
                        pe.wait_ge(S["ffn_loaded"], lin(ch, lambda c: 48 * (c - FIRST_FFN + 1)))
                    for k in range(CT):
                        mm = pe.transpose(t[:, k * P:(k + 1) * P], xe[:, th * CT + k, :], ident)
                elif name[0] == "h":
                    th, f = int(name[1]), int(name[2])
                    pe.wait_ge(*tile_read(ch, f"xt{th}"))
                    mm = pe.matmul(t[:, :], w1_sb[:, f * P:(f + 1) * P], xeT[:, th * CH:(th + 1) * CH],
                                   start=True, stop=True)
                else:
                    th = int(name[1])
                    if part == 0:
                        pe.wait_ge(*tile_read(ch, f"h{th}{FT - 1}"))
                    for f in range(FT):
                        mm = pe.matmul(t[:, part * P:(part + 1) * P], hT[:, f, part * P:(part + 1) * P],
                                       w2_sb[:, f, :], start=(f == 0), stop=(f == FT - 1))
                if name[0] != "o" or part == CT - 1:
                    mm.then_inc(S["misc_pe"], 1)

            def spread_du(ch, w):
                hf = w // UNITS
                if w % UNITS == 0:
                    pe.wait_ge(S["stacked"], per_chunk(ch, 128, 64 * (hf + 1)))
                wait(pe, "u_ready", per_chunk(ch, SLOTS, w - 1))
                pe.matmul(du_ps[w % 2][:, :], sel_d[:, group_of(w), :, :].rearrange("k n d -> k (n d)"),
                          dsp[:, hf, head_of(w), 1, :], start=True, stop=True).then_inc(S["du_spread"], 1)

            def spread_delta(ch, w):
                last = w - 2 if w >= 3 else (-1, 0, -2)[w]
                wait(pe, "scan_done", per_chunk(ch, SLOTS, last))
                pe.matmul(decay_of(w)[:, :], sel_d[:, group_of(w), :, :].rearrange("k n d -> k (n d)"),
                          dsp[:, w // UNITS, head_of(w), 0, :], start=True, stop=True
                          ).then_inc(S["delta_spread"], 1)

            def spread(ch, w):
                spread_du(ch, w)
                spread_delta(ch, w)

            def sum_quad(ch, k):
                r = k % (UNITS // QUADS)
                if r == 0:
                    wait(pe, "y_read", per_chunk(ch, 2, k * QUADS // UNITS))
                wait_products(pe, ch, QUADS * (k + 1))
                for q in range(QUADS):
                    mm = pe.matmul(y_ps[q * 32:(q + 1) * 32, :], con[:, K_SUM + 32 * r:K_SUM + 32 * (r + 1)],
                                   s_sb[:, (QUADS * k + q) % S_RING, :],
                                   start=(r == 0), stop=(r == UNITS // QUADS - 1))
                mm.then_inc(S["sum_done"], 1)

            first, start = (0, None), (-1, None)
            pe.wait_ge(S["xnT_act"], CHUNKS)
            def in_projs(hf):
                in_proj(first, start, f"z{hf}", 0)
                for k in range(TAPS):
                    in_proj(first, start, f"x{hf}", k)

            in_projs(0)
            x_proj(first, start, "bc0")
            x_proj(first, start, "v0")
            pe.wait_ge(S["route_dve"], 1)
            pe.matmul(du_ps[0][:, :], tri, rt_hot, start=True, stop=True)
            pe.matmul(du_ps[1][:, :], ones, rt_hot, start=True, stop=True).then_inc(S["route_pe"], 1)
            in_projs(1)
            for name in ("B0", "B1", "C0", "C1"):
                spread_bc(first, start, name)
            x_proj(first, start, "bc1")
            x_proj(first, start, "v1")
            pe.wait_ge(S["route_dve"], 2)
            for w in range(AHEAD):
                spread(first, w)

            def body(ch):
                plan = tiles_of(ch[0])
                for w in range(SLOTS):
                    if w + AHEAD < SLOTS:
                        spread(ch, w + AHEAD)
                    elif ch[0] + 1 < CHUNKS:
                        spread(after(ch), w + AHEAD - SLOTS)
                    if (w - SUM) % QUADS == 0:
                        if w >= SUM:
                            sum_quad(ch, (w - SUM) // QUADS)
                        elif ch[0] > 0:
                            sum_quad(before(ch), (w - SUM) // QUADS + SLOTS // QUADS)
                    for slots, name, _ in plan:
                        for part in [k for k, slot in enumerate(slots) if slot == w]:
                            if name[0] in "xz" and name[1] in "01":
                                in_proj(after(ch), ch, name, part)
                            elif name[0] in "BC":
                                spread_bc(ch if int(name[1]) > 1 else after(ch), ch, name)
                            elif name[0] in "bv":
                                x_proj(after(ch), ch, name)
                            elif name == "outp":
                                out_proj(before(ch), tile_bank(ch, name) if part else claim(ch, name), part)
                            else:
                                expert(ch, name, part)

            def last():
                end = (CHUNKS - 1, None)
                sum_quad(end, SLOTS // QUADS - 1)
                pe.wait_ge(S["misc_act"], base["misc_act"][CHUNKS + 1])
                pe.wait_ge(S["misc_dve"], base["misc_dve"][CHUNKS + 1])
                out_proj(end, misc[0], 0)
                out_proj(end, misc[0], 1)

            chunks(pe, body, last)


_INS = ["L0_attn_hidden_states", "L0_attn_in_proj_w", "L0_attn_conv_w", "L0_attn_conv_b",
        "L0_attn_x_proj_w", "L0_attn_dt_proj_w", "L0_attn_dt_proj_b", "L0_attn_A_log", "L0_attn_Dskip",
        "L0_attn_out_proj_w", "L0_ffn_Wg", "L0_ffn_W1", "L0_ffn_b1", "L0_ffn_W2", "L0_ffn_b2"]


def _constants(np):
    c = np.zeros((P, K_ALL), np.float32)
    k = np.arange(P)
    c[:, K_ID:K_ID + P] = np.eye(P)
    c[:, K_TRI:K_TRI + P] = k[:, None] <= k[None, :]
    c[:, K_I2:K_I2 + 64] = (k[:, None] % 64) == np.arange(64)[None, :]
    for r in range(4):
        c[:, K_SUM + 32 * r:K_SUM + 32 * (r + 1)] = k[:, None] % UC + UC * r == np.arange(32)[None, :]
    col = np.arange(EXP * TILES)
    c[:, K_KEEP:K_KEEP + EXP * TILES] = col % TILES != 0
    c[:, K_BASE:K_ALL] = col // TILES * CAP
    c[:, K_FIRST:K_FIRST + EXP] = EXP - np.arange(EXP)
    c[:, K_TRASH:K_TRASH + TILES] = TOK + np.arange(TILES)[None, :] * P + k[:, None]
    c[:, K_ONE:K_ONE + P] = 1.0
    return c


def kernel(**inputs):
    import numpy as np
    import concourse.bacc as bacc
    from concourse.bass_utils import run_bass_kernel_spmd

    nc = bacc.Bacc("TRN2", target_bir_lowering=False, num_devices=1)
    flat = {"L0_attn_hidden_states": (TOK, DM), "L0_attn_conv_w": (DIN, TAPS),
            "L0_ffn_W1": (EXP * DM, FF), "L0_ffn_W2": (EXP * FF, DM)}
    arrays, args = {}, []
    for name in _INS + ["consts"]:
        a = _constants(np) if name == "consts" else np.ascontiguousarray(inputs[name])
        a = a.reshape(flat.get(name, a.shape))
        arrays[name] = a
        args.append(nc.dram_tensor(name, a.shape, mybir.dt.from_np(a.dtype), kind="ExternalInput").ap())
    out = nc.dram_tensor("out", (TOK, DM), F32, kind="ExternalOutput").ap()
    bass_mamba_moe(nc, *args, out)
    r = run_bass_kernel_spmd(nc, [arrays], core_ids=[0])
    return r.results[0]["out"].reshape(BATCH, SEQ, DM)
```
